# Optimizing a Trainium2 kernel written in Bass

```python
import numpy as np
import jax
import jax.numpy as jnp

def _softmax(x, axis=-1):
    return jax.nn.softmax(x, axis=axis)

def _gelu(x):
    return jax.nn.gelu(x, approximate=True)

def _silu(x):
    return jax.nn.silu(x)

def _sigmoid(x):
    return jax.nn.sigmoid(x)

def _layernorm(x, axis=-1, eps=1e-05):
    m = jnp.mean(x, axis=axis, keepdims=True)
    v = jnp.var(x, axis=axis, keepdims=True)
    return (x - m) / jnp.sqrt(v + eps)

def _scatter_add(tgt, idx, src, axis=0):
    return tgt.at[idx].add(src)

def _segment_sum(src, seg, n):
    return jax.ops.segment_sum(src, seg, n)
kernel_name = 'mk_gnn_resnorm_d2_gnn_r8_d623a8'

def setup_inputs(seed: int=0):
    np.random.seed(seed)
    _w = jnp.asarray

    def _rec_inputs():
        import jax
        import jax.numpy as jnp
        _gk = jax.random.key(seed)
        x = -1.686e-05 + 1 * jax.random.normal(jax.random.fold_in(_gk, 1), (12500, 160), jnp.float32)
        _s = jax.random.randint(jax.random.fold_in(_gk, 2), (100000,), 0, 12500, jnp.int32)
        _d = jax.random.randint(jax.random.fold_in(_gk, 3), (100000,), 0, 12500, jnp.int32)
        _loop = jnp.arange(12500, dtype=jnp.int32)
        src = jnp.concatenate([_s, _d, _loop])
        dst = jnp.concatenate([_d, _s, _loop])
        _o = jnp.argsort(dst, stable=True)
        src = src[_o]
        dst = dst[_o]
        edge_attr_16 = -0.000191324 + 0.999809 * jax.random.normal(jax.random.fold_in(_gk, 12), (212500, 16), jnp.float32)
        edge_attr_4 = 0.0007022 + 0.999661 * jax.random.normal(jax.random.fold_in(_gk, 13), (212500, 4), jnp.float32)
        node_vec1 = -0.00915711 + 0.999674 * jax.random.normal(jax.random.fold_in(_gk, 15), (12500, 1), jnp.float32)
        return (x, src, dst, edge_attr_16, edge_attr_4, node_vec1)
    x, src, dst, edge_attr_16, edge_attr_4, node_vec1 = _rec_inputs()

    def _L0_gnn_setup():
        import jax, jax.numpy as jnp
        import numpy as np
        MUL0, MUL1 = (64, 32)
        INV_SQRT3 = 1.0 / np.sqrt(3.0)

        def _split(x):
            return (x[:, :MUL0], x[:, MUL0:].reshape(x.shape[0], MUL1, 3))

        def _merge(o0, o1):
            return jnp.concatenate([o0, o1.reshape(o1.shape[0], -1)], axis=-1)

        def _tp(x0, x1, y0, y1, w000, w011, w101, w110):
            fan0 = x0.shape[1] * y0.shape[1] + x1.shape[1] * y1.shape[1]
            fan1 = x0.shape[1] * y1.shape[1] + x1.shape[1] * y0.shape[1]
            out0 = (jnp.einsum('eu,ev,uvw->ew', x0, y0, w000) + INV_SQRT3 * jnp.einsum('euk,evk,uvw->ew', x1, y1, w110)) / np.sqrt(fan0)
            out1 = (jnp.einsum('eu,evk,uvw->ewk', x0, y1, w011) + jnp.einsum('euk,ev,uvw->ewk', x1, y0, w101)) / np.sqrt(fan1)
            return (out0, out1)

        def _lin(x0, x1, w0, w1):
            return (x0 @ w0 / np.sqrt(x0.shape[1]), jnp.einsum('euk,uv->evk', x1, w1) / np.sqrt(x1.shape[1]))
        key = jax.random.key(seed)
        ks = jax.random.split(key, 20)
        N, E = (6250, 62500)
        inp = {'node_features': jax.random.normal(ks[0], (N, MUL0 + 3 * MUL1), dtype=jnp.float32), 'edge_index': jax.random.randint(ks[1], (2, E), 0, N, dtype=jnp.int64), 'edge_attr_tensor': jax.random.normal(ks[2], (E, 4), dtype=jnp.float32), 'node_attr_scalar_raw': jax.random.normal(ks[3], (N, 1), dtype=jnp.float32), 'wm000': jax.random.normal(ks[4], (MUL0, 1, MUL0), dtype=jnp.float32), 'wm011': jax.random.normal(ks[5], (MUL0, 1, MUL1), dtype=jnp.float32), 'wm101': jax.random.normal(ks[6], (MUL1, 1, MUL1), dtype=jnp.float32), 'wm110': jax.random.normal(ks[7], (MUL1, 1, MUL0), dtype=jnp.float32), 'lm0': jax.random.normal(ks[8], (MUL0, MUL0), dtype=jnp.float32), 'lm1': jax.random.normal(ks[9], (MUL1, MUL1), dtype=jnp.float32), 'wu000': jax.random.normal(ks[10], (MUL0, MUL0, MUL0), dtype=jnp.float32), 'wu011': jax.random.normal(ks[11], (MUL0, MUL1, MUL1), dtype=jnp.float32), 'wu101': jax.random.normal(ks[12], (MUL1, MUL0, MUL1), dtype=jnp.float32), 'wu110': jax.random.normal(ks[13], (MUL1, MUL1, MUL0), dtype=jnp.float32), 'lu0': jax.random.normal(ks[14], (MUL0, MUL0), dtype=jnp.float32), 'lu1': jax.random.normal(ks[15], (MUL1, MUL1), dtype=jnp.float32)}
        return inp
    _L0_gnn_all = _L0_gnn_setup()
    _L0_gnn_in = {k: v for k, v in _L0_gnn_all.items() if k in ('wm000', 'wm011', 'wm101', 'wm110', 'lm0', 'lm1', 'wu000', 'wu011', 'wu101', 'wu110', 'lu0', 'lu1')}
    del _L0_gnn_all

    def _L1_gnn_setup():
        import jax, jax.numpy as jnp
        import numpy as np
        N = 2500
        E = 40000
        MUL0 = 64
        MUL1 = 32
        FC_IN = 16
        FC_H = 64
        WNUM = 192
        key = jax.random.key(seed)
        ks = jax.random.split(key, 16)
        return {'x': jax.random.normal(ks[0], (N, MUL0 + 3 * MUL1), jnp.float32), 'node_attr': jnp.ones((N, 1), jnp.float32), 'edge_scalars': jax.random.normal(ks[1], (E, FC_IN), jnp.float32), 'edge_attr_sh': jax.random.normal(ks[2], (E, 4), jnp.float32), 'edge_src': jax.random.randint(ks[3], (E,), 0, N), 'edge_dst': jax.random.randint(ks[4], (E,), 0, N), 'Wfc1': jax.random.normal(ks[5], (FC_IN, FC_H), jnp.float32), 'Wfc2': jax.random.normal(ks[6], (FC_H, WNUM), jnp.float32), 'Wsc0': jax.random.normal(ks[7], (MUL0, MUL0), jnp.float32), 'Wsc1': jax.random.normal(ks[8], (MUL1, MUL1), jnp.float32), 'Wl1_0': jax.random.normal(ks[9], (MUL0, MUL0), jnp.float32), 'Wl1_1': jax.random.normal(ks[10], (MUL1, MUL1), jnp.float32), 'Wl2_s': jax.random.normal(ks[11], (MUL0 + MUL1, MUL0), jnp.float32), 'Wl2_v': jax.random.normal(ks[12], (MUL0 + MUL1, MUL1), jnp.float32), 'Wa': 0.1 * jax.random.normal(ks[13], (MUL0 + MUL1, 1), jnp.float32)}
    _L1_gnn_all = _L1_gnn_setup()
    _L1_gnn_in = {k: v for k, v in _L1_gnn_all.items() if k in ('Wfc1', 'Wfc2', 'Wsc0', 'Wsc1', 'Wl1_0', 'Wl1_1', 'Wl2_s', 'Wl2_v', 'Wa')}
    del _L1_gnn_all
    return {'x': x, 'src': src, 'dst': dst, 'edge_attr_16': edge_attr_16, 'edge_attr_4': edge_attr_4, 'node_vec1': node_vec1, 'L0_gnn_wm000': _L0_gnn_in['wm000'], 'L0_gnn_wm011': _L0_gnn_in['wm011'], 'L0_gnn_wm101': _L0_gnn_in['wm101'], 'L0_gnn_wm110': _L0_gnn_in['wm110'], 'L0_gnn_lm0': _L0_gnn_in['lm0'], 'L0_gnn_lm1': _L0_gnn_in['lm1'], 'L0_gnn_wu000': _L0_gnn_in['wu000'], 'L0_gnn_wu011': _L0_gnn_in['wu011'], 'L0_gnn_wu101': _L0_gnn_in['wu101'], 'L0_gnn_wu110': _L0_gnn_in['wu110'], 'L0_gnn_lu0': _L0_gnn_in['lu0'], 'L0_gnn_lu1': _L0_gnn_in['lu1'], 'L1_gnn_Wfc1': _L1_gnn_in['Wfc1'], 'L1_gnn_Wfc2': _L1_gnn_in['Wfc2'], 'L1_gnn_Wsc0': _L1_gnn_in['Wsc0'], 'L1_gnn_Wsc1': _L1_gnn_in['Wsc1'], 'L1_gnn_Wl1_0': _L1_gnn_in['Wl1_0'], 'L1_gnn_Wl1_1': _L1_gnn_in['Wl1_1'], 'L1_gnn_Wl2_s': _L1_gnn_in['Wl2_s'], 'L1_gnn_Wl2_v': _L1_gnn_in['Wl2_v'], 'L1_gnn_Wa': _L1_gnn_in['Wa']}

def reference(x, src, dst, edge_attr_16, edge_attr_4, node_vec1, L0_gnn_wm000, L0_gnn_wm011, L0_gnn_wm101, L0_gnn_wm110, L0_gnn_lm0, L0_gnn_lm1, L0_gnn_wu000, L0_gnn_wu011, L0_gnn_wu101, L0_gnn_wu110, L0_gnn_lu0, L0_gnn_lu1, L1_gnn_Wfc1, L1_gnn_Wfc2, L1_gnn_Wsc0, L1_gnn_Wsc1, L1_gnn_Wl1_0, L1_gnn_Wl1_1, L1_gnn_Wl2_s, L1_gnn_Wl2_v, L1_gnn_Wa):
    import jax
    import jax.numpy as jnp

    def _L0_gnn_ref(node_features, edge_index, edge_attr_tensor, node_attr_scalar_raw, wm000, wm011, wm101, wm110, lm0, lm1, wu000, wu011, wu101, wu110, lu0, lu1):
        import jax, jax.numpy as jnp
        import numpy as np
        MUL0, MUL1 = (64, 32)
        INV_SQRT3 = 1.0 / np.sqrt(3.0)

        def _split(x):
            return (x[:, :MUL0], x[:, MUL0:].reshape(x.shape[0], MUL1, 3))

        def _merge(o0, o1):
            return jnp.concatenate([o0, o1.reshape(o1.shape[0], -1)], axis=-1)

        def _tp(x0, x1, y0, y1, w000, w011, w101, w110):
            fan0 = x0.shape[1] * y0.shape[1] + x1.shape[1] * y1.shape[1]
            fan1 = x0.shape[1] * y1.shape[1] + x1.shape[1] * y0.shape[1]
            out0 = (jnp.einsum('eu,ev,uvw->ew', x0, y0, w000) + INV_SQRT3 * jnp.einsum('euk,evk,uvw->ew', x1, y1, w110)) / np.sqrt(fan0)
            out1 = (jnp.einsum('eu,evk,uvw->ewk', x0, y1, w011) + jnp.einsum('euk,ev,uvw->ewk', x1, y0, w101)) / np.sqrt(fan1)
            return (out0, out1)

        def _lin(x0, x1, w0, w1):
            return (x0 @ w0 / np.sqrt(x0.shape[1]), jnp.einsum('euk,uv->evk', x1, w1) / np.sqrt(x1.shape[1]))
        N = node_features.shape[0]
        row, col = (edge_index[0], edge_index[1])
        r_vec = edge_attr_tensor[:, :3]
        dist = edge_attr_tensor[:, 3:4]
        e0 = dist
        e1 = r_vec[:, None, :]
        xj0, xj1 = _split(node_features[col])
        m0, m1 = _tp(xj0, xj1, e0, e1, wm000, wm011, wm101, wm110)
        d0, d1 = _lin(xj0, xj1, lm0, lm1)
        msgs = _merge(m0 + d0, m1 + d1)
        agg = jax.ops.segment_sum(msgs, row, num_segments=N)
        a0, a1 = _split(agg)
        x0, x1 = _split(node_features)
        u0, u1 = _tp(x0, x1, a0, a1, wu000, wu011, wu101, wu110)
        ud0, ud1 = _lin(x0, x1, lu0, lu1)
        return node_features + _merge(u0 + ud0, u1 + ud1)

    def _L1_gnn_ref(x, node_attr, edge_scalars, edge_attr_sh, edge_src, edge_dst, Wfc1, Wfc2, Wsc0, Wsc1, Wl1_0, Wl1_1, Wl2_s, Wl2_v, Wa):
        import jax, jax.numpy as jnp
        import numpy as np
        N = 2500
        E = 40000
        MUL0 = 64
        MUL1 = 32
        FC_IN = 16
        FC_H = 64
        WNUM = 192
        n = x.shape[0]
        x0 = x[:, :MUL0]
        x1 = x[:, MUL0:].reshape(n, MUL1, 3)
        a = node_attr
        h = jax.nn.silu(edge_scalars @ (Wfc1 / jnp.sqrt(jnp.float32(FC_IN))))
        w = h @ (Wfc2 / jnp.sqrt(jnp.float32(FC_H)))
        w0 = w[:, :64]
        w1 = w[:, 64:128]
        w2 = w[:, 128:160]
        w3 = w[:, 160:192]
        inv8 = 1.0 / jnp.sqrt(jnp.float32(MUL0))
        inv32 = 1.0 / jnp.sqrt(jnp.float32(MUL1))
        sc = jnp.concatenate([x0 @ Wsc0 * a * inv8, (jnp.einsum('num,uv->nvm', x1, Wsc1) * a[..., None] * inv32).reshape(n, 3 * MUL1)], axis=1)
        f0 = x0 @ Wl1_0 * a * inv8
        f1 = jnp.einsum('num,uv->nvm', x1, Wl1_1) * a[..., None] * inv32
        e0 = f0[edge_src]
        e1 = f1[edge_src]
        sh0 = edge_attr_sh[:, :1]
        sh1 = edge_attr_sh[:, 1:4]
        mid0 = w0 * e0 * sh0
        mid1 = w3 * jnp.einsum('eum,em->eu', e1, sh1) / jnp.sqrt(3.0)
        mid2 = w1[:, :, None] * e0[:, :, None] * sh1[:, None, :]
        mid3 = w2[:, :, None] * e1 * sh0[:, :, None]
        cnt = jnp.clip(jax.ops.segment_sum(jnp.ones(edge_dst.shape, x.dtype), edge_dst, num_segments=n), 1.0)

        def smean(v):
            s = jax.ops.segment_sum(v, edge_dst, num_segments=n)
            return s / cnt.reshape((n,) + (1,) * (v.ndim - 1))
        n0, n1 = (smean(mid0), smean(mid1))
        n2, n3 = (smean(mid2), smean(mid3))
        scal = jnp.concatenate([n0, n1], axis=1)
        vec = jnp.concatenate([n2, n3], axis=1)
        inv96 = 1.0 / jnp.sqrt(jnp.float32(MUL0 + MUL1))
        alpha = scal @ Wa * a * inv96
        out_s = scal @ Wl2_s * a * inv96
        out_v = jnp.einsum('num,uv->nvm', vec, Wl2_v) * a[..., None] * inv96
        conv = jnp.concatenate([out_s, out_v.reshape(n, 3 * MUL1)], axis=1)
        return sc + alpha * conv
    edge_index = jnp.stack([src, dst])
    x = _layernorm(x + _L0_gnn_ref(x, edge_index, edge_attr_4, node_vec1, L0_gnn_wm000, L0_gnn_wm011, L0_gnn_wm101, L0_gnn_wm110, L0_gnn_lm0, L0_gnn_lm1, L0_gnn_wu000, L0_gnn_wu011, L0_gnn_wu101, L0_gnn_wu110, L0_gnn_lu0, L0_gnn_lu1), axis=-1)
    x = _layernorm(x + _L1_gnn_ref(x, node_vec1, edge_attr_16, edge_attr_4, src, dst, L1_gnn_Wfc1, L1_gnn_Wfc2, L1_gnn_Wsc0, L1_gnn_Wsc1, L1_gnn_Wl1_0, L1_gnn_Wl1_1, L1_gnn_Wl2_s, L1_gnn_Wl2_v, L1_gnn_Wa), axis=-1)
    return x

_drawn_inputs = setup_inputs


def setup_inputs(seed=0):
    import zlib

    import numpy as np

    out = dict(_drawn_inputs(seed))
    spreads = {}
    factors = {'edge_attr_16': 8.0,
     'L1_gnn_Wfc1': 8.0,
     'L1_gnn_Wfc2': 8.0,
     'L1_gnn_Wl1_0': 8.0,
     'L1_gnn_Wl1_1': 8.0,
     'L1_gnn_Wl2_s': 8.0,
     'L1_gnn_Wl2_v': 8.0,
     'L1_gnn_Wa': 8.0}
    for name, (base, spread) in spreads.items():
        noise = np.random.default_rng([zlib.crc32(name.encode()), seed]).standard_normal(out[name].shape)
        drawn = base * np.exp(spread * noise) if base else spread * noise
        out[name] = jnp.asarray(drawn.astype(out[name].dtype))
    for name, factor in factors.items():
        out[name] = (out[name] * factor).astype(out[name].dtype)
    return out
```

```python
import concourse.bass as bass
from concourse import mybir
from contextlib import ExitStack
import numpy as np

N, D, E = 12500, 160, 212500
S0, V0 = 64, 32
P = 128
FULL = E // P
TAIL = E - P * FULL
HALF = 4
RING = 2 * HALF
STEPS = -(-(FULL + 1) // RING)
T = STEPS * RING
NP = 125
NT = N // NP
ROWS = N + 172
RPP = ROWS // P
DP = D + D + 3 * S0 + V0
DM = 4 * 96 + 1
ACC0, ACC1 = 4, 2
Z0, Z1 = 3960, 3465
C0 = RPP * D // Z0
C1 = RPP * DM // Z1
assert C0 * Z0 == RPP * D and C1 * Z1 == RPP * DM and NT * NP == N and T * P >= E
I3, F96, F5120, F4096 = 1 / np.sqrt(3.0), 1 / np.sqrt(96.0), 1 / np.sqrt(5120.0), 1 / 64.0
R32 = 1 / np.sqrt(32.0)
EPS = 1e-5


def program(nc, x, src, dst, attr16, attr4, nvec, wm000, wm011, wm101, wm110, lm0, lm1,
            wu000, wu011, wu101, wu110, lu0, lu1, wfc1, wfc2, wsc0, wsc1, wl10, wl11, wl2s, wl2v, wa, out):
    f32, i32, u32 = mybir.dt.float32, mybir.dt.int32, mybir.dt.uint32
    ALU, ACT, AX = mybir.AluOpType, mybir.ActivationFunctionType, mybir.AxisListType
    ctx = ExitStack()
    with ctx:
        def sb(name, shape, dt=f32):
            return ctx.enter_context(nc.sbuf_tensor(name, shape, dt))

        def sem(name):
            return ctx.enter_context(nc.semaphore(name))

        def sems(name, n):
            return [sem(f"{name}{i}") for i in range(n)]

        def dram(name, shape):
            return nc.dram_tensor(name, shape, f32, kind="Internal").ap()

        prodtab = dram("prodtab", [N, DP])
        normed = dram("normed", [N, D])
        ftab = dram("ftab", [N, D])
        basetab = dram("basetab", [N, D])
        acc0 = [dram(f"acc0_{c}", [ROWS, D]) for c in range(ACC0)]
        acc1 = [dram(f"acc1_{c}", [ROWS, DM]) for c in range(ACC1)]

        ident = sb("ident", [P, P])
        before = sb("before", [P, P])
        ones = sb("ones", [P, P])
        trash = sb("trash", [P, 1])
        trash_i = sb("trash_i", [P, 1], i32)
        eps = sb("eps", [P, 1])
        W0 = sb("W0", [S0, 160])
        W1 = sb("W1", [96, 96 + 96 + 3 * S0])
        WU0 = sb("WU0", [S0, S0 * S0])
        WU011 = sb("WU011", [S0, V0 * V0])
        WU101 = sb("WU101", [S0, V0 * V0])
        WU110 = sb("WU110", [P, 8, S0])
        LU0 = sb("LU0", [S0, S0])
        LU1 = sb("LU1", [96, 96])
        WN0 = sb("WN0", [S0, 2, S0])
        WN1 = sb("WN1", [96, 2, 96])
        WF1 = sb("WF1", [HALF * 16, 2, P])
        WF2 = sb("WF2", [P, 192])
        WS = sb("WS", [96, 1 + S0])
        WV = sb("WV", [96, V0])

        src_i = sb("src_i", [P, T + RING], i32)
        dst_i = sb("dst_i", [P, T + RING], i32)
        src_f = sb("src_f", [P, T])
        dst_f = sb("dst_f", [P, T])
        sh = sb("sh", [P, T * 4])

        xin = sb("xin", [NP, 2, D])
        xc = sb("xc", [NP, 2, D])
        xT = sb("xT", [96, 2, 3 * NP])
        nv = sb("nv", [NP, 2])
        nout = sb("nout", [NP, 2, DP])
        arena = sb("arena", [P, 3 * S0 * V0])
        zs = sb("zs", [P, S0 * S0])
        zz = sb("zz", [NP, 3, V0, V0])
        zzT = sb("zzT", [P, 8 * NP])
        agg = sb("agg", [NP, 2, 2 * DM])
        pair = sb("pair", [NP, 2, D])
        ac = sb("ac", [NP, 2, D])
        r0 = sb("r0", [NP, S0])
        r1 = sb("r1", [NP, 96])
        y = sb("y", [NP, D])
        st6 = sb("st6", [NP, 6])
        mv = sb("mv", [NP, 2])
        sd = sb("sd", [NP, 1])
        rstd = sb("rstd", [NP, 1])
        summed = sb("summed", [NP, 2, DM])
        sumT = sb("sumT", [96, 2, 4 * NP])
        gain = sb("gain", [NP, 4])

        gathered0 = arena[:, 0:RING * DP].rearrange("p (j d) -> p j d", j=RING)
        gathered1 = arena[:, 0:RING * D].rearrange("p (j d) -> p j d", j=RING)
        gidx = sb("gidx", [P, RING], i32)
        sidx = sb("sidx", [P, RING], i32)
        keyc = sb("keyc", [P, RING])
        shc = sb("shc", [P, RING * 4])
        toff = sb("toff", [P, RING])
        prev = sb("prev", [P, RING])
        moved = sb("moved", [P, RING])
        same = sb("same", [P, 2, P])
        junk = sb("junk", [P, P])
        PARTS = DM + 2 * V0
        parts = sb("parts", [P, 2, PARTS])
        sums = sb("sums", [P, RING, DM])
        es = sb("es", [P, 2, HALF * 16])
        esT = sb("esT", [HALF * 16, P])
        hT = sb("hT", [P, 2, P])

        bank = [ctx.enter_context(nc.psum_tensor(f"bank{i}", [P, 512], f32)) for i in range(8)]

        w_in = sem("w_in")
        w_const = sem("w_const")
        w_zero = sem("w_zero")
        w_pad = sem("w_pad")
        w_ready = sem("w_ready")
        w_step = sem("w_step")
        a_in, a_xc, a_T, a_Ts, a_mm, a_out, a_st = (sems("a_in", 2), sem("a_xc"), sem("a_T"), sem("a_Ts"), sem("a_mm"),
                                                    sem("a_out"), sems("a_st", 2))
        stage_b, stage_e = [dict(gath=sems(s + "_gath", RING), used=sem(s + "_used"), key=sem(s + "_key"),
                                 kT=sem(s + "_kT"), same=sem(s + "_same"), parts=sem(s + "_parts"),
                                 sum=sem(s + "_sum"), out=sem(s + "_out"), sidx=sem(s + "_sidx"), tmp=sem(s + "_tmp"))
                            for s in "be"]
        settled0 = sems("settled0_", ACC0)
        settled1 = sems("settled1_", ACC1)
        e_es, e_esT, e_esTs, e_h, e_hs, e_w = (sems("e_es", 2), sem("e_esT"), sem("e_esTs"), sem("e_h"), sem("e_hs"),
                                               sem("e_w"))
        c_in, c_pair, c_prep, c_zz, c_T, c_Ts, c_Y, c_Yused = (sems("c_in", 2), sem("c_pair"), sem("c_prep"), sem("c_zz"),
                                                               sem("c_T"), sem("c_Ts"), sem("c_Y"), sem("c_Yused"))
        c_zT, c_zTs, c_R, c_red, c_v, c_var, c_sd, c_xn, c_st = (sem("c_zT"), sem("c_zTs"), sem("c_R"), sem("c_red"),
                                                                 sem("c_v"), sem("c_var"), sem("c_sd"), sem("c_xn"),
                                                                 sems("c_st", 2))
        d_in, d_T, d_Ts, d_mm, d_out, d_st = (sems("d_in", 2), sem("d_T"), sem("d_Ts"), sem("d_mm"), sem("d_out"),
                                              sems("d_st", 2))
        f_in, f_sum, f_T, f_Ts, f_mm, f_v, f_var, f_sd, f_out, f_st = (
            sems("f_in", 2), sem("f_sum"), sem("f_T"), sem("f_Ts"), sem("f_mm"), sem("f_v"), sem("f_var"), sem("f_sd"),
            sem("f_out"), sems("f_st", 2))
        block = ctx.enter_context(nc.Block())

        def wait(eng, s, v):
            if not isinstance(v, int) or v > 0:
                eng.wait_ge(s, v)

        def wait_adds(eng, s, clears, adds):
            eng.wait_ge(s, 16 * (clears + (max(adds, 0) if isinstance(adds, int) else adds)))

        def plain(eng):
            eng.sem_inc(w_step, 1)

        def looped(eng, count, body):
            body(0)
            with eng.Fori(1, count) as i:
                body(i)

        def rows(tensor, n):
            return tensor[bass.ds(n * NP, NP), :]

        def blocks3(t, c0, w):
            return [t[32 * k:32 * k + 32, c0 + w * k:c0 + w * k + w] for k in range(3)]

        WN1f = WN1[:, :, :].rearrange("p a n -> p (a n)")
        loads = [
            (W0[:, 0:64], lm0), (W0[:, 64:128], wm000.rearrange("u a w -> u (a w)")),
            (W0[:, 128:160], wm011.rearrange("u a w -> u (a w)")),
            (WU0[:, :], wu000.rearrange("u v w -> u (v w)")), (WU011[:, :], wu011.rearrange("u v w -> u (v w)")),
            (WU101[:, :].rearrange("v (u w) -> v u w", u=V0), wu101.rearrange("u v w -> v u w")),
            (WU110[:, :, :], wu110.rearrange("u v w -> (u v) w").rearrange("(c p) w -> p c w", p=P)),
            (LU0[:, :], lu0), (WN0[:, 0, :], wl10), (WN0[:, 1, :], wsc0),
            (WF2[0:64, :], wfc2), (WF2[64:128, :], wfc2), (WS[:, 1:65], wl2s), (WV[:, :], wl2v),
            (src_i[:, 0:FULL], src[0:P * FULL].rearrange("(p t) -> p t", p=P)),
            (dst_i[:, 0:FULL], dst[0:P * FULL].rearrange("(p t) -> p t", p=P)),
            (src_i[0:TAIL, FULL:FULL + 1], src[P * FULL:E].rearrange("(p t) -> p t", t=1)),
            (dst_i[0:TAIL, FULL:FULL + 1], dst[P * FULL:E].rearrange("(p t) -> p t", t=1)),
            (sh[:, 0:FULL * 4], attr4[0:P * FULL, :].rearrange("(p t) a -> p (t a)", p=P)),
            (sh[0:TAIL, FULL * 4:FULL * 4 + 4], attr4[P * FULL:E, :]),
            (WS[:, 0:1], wa),
        ]
        loads += [(b, lm1) for b in blocks3(W1, 0, 32)]
        loads += [(b, wm101.rearrange("u a w -> u (a w)")) for b in blocks3(W1, 96, 32)]
        loads += [(b, wm110.rearrange("u a w -> u (a w)")) for b in blocks3(W1, 192, 64)]
        loads += [(b, lu1) for b in blocks3(LU1, 0, 32)]
        loads += [(b, wl11) for b in blocks3(WN1f, 0, 32)]
        loads += [(b, wsc1) for b in blocks3(WN1f, 96, 32)]
        loads += [(WF1[16 * j:16 * j + 16, j // 2, 64 * (j % 2):64 * (j % 2) + 64], wfc1) for j in range(HALF)]
        WIN = 16 * len(loads)

        attr16_v = attr16[0:P * FULL, :].rearrange("(p t) a -> p (t a)", p=P)
        HW = HALF * 16

        attr16_v = attr16[0:P * FULL, :].rearrange("(p t) a -> p (t a)", p=P)
        HW = HALF * 16

        def node_traffic(sp, load, out_ready, store):
            load(0, 0)
            load(1, 1)
            with sp.Fori(0, NT // 2 - 1) as h:
                for b in range(2):
                    sp.wait_ge(out_ready, 2 * h + b + 1)
                    store(2 * h + b, b)
                    load(2 * h + b + 2, b)
            for b in range(2):
                sp.wait_ge(out_ready, NT - 1 + b)
                store(NT - 2 + b, b)

        @block.sync
        def _(sp):
            sp.wait_ge(w_zero, 1)
            for to, frm in loads:
                sp.dma_start(to, frm).then_inc(w_in, 16)

            node_traffic(sp, lambda n, b: sp.dma_start(xin[:, b, :], rows(x, n)).then_inc(a_in[b], 16), a_out,
                         lambda n, b: sp.dma_start(rows(prodtab, n), nout[:, b, :]).then_inc(a_st[b], 16))

            for c in range(ACC0):
                sp.wait_ge(settled0[c], 16 * (C0 + T // ACC0))

            def load_c(n, b):
                sp.dma_start(xin[:, b, :], rows(x, n)).then_inc(c_in[b], 16)
                for c in range(ACC0):
                    sp.dma_start(agg[:, b, c * D:(c + 1) * D], rows(acc0[c], n)).then_inc(c_in[b], 16)

            node_traffic(sp, load_c, c_xn,
                         lambda n, b: sp.dma_start(rows(normed, n), nout[:, b, 0:D]).then_inc(c_st[b], 16))

            for b in range(2):
                sp.wait_ge(c_st[b], 16 * (NT // 2))

            def load_d(n, b):
                sp.dma_start(xin[:, b, :], rows(normed, n)).then_inc(d_in[b], 16)
                sp.dma_start(nv[:, b:b + 1], rows(nvec, n)).then_inc(d_in[b], 16)

            def store_d(n, b):
                sp.dma_start(rows(ftab, n), nout[:, b, 0:D]).then_inc(d_st[b], 16)
                sp.dma_start(rows(basetab, n), nout[:, b, D:2 * D]).then_inc(d_st[b], 16)

            node_traffic(sp, load_d, d_out, store_d)

            def load_e(i):
                for q in range(2):
                    wait(sp, e_esT, 2 * i + q - 1)
                    sp.dma_start(es[:, q, :], attr16_v[:, bass.ds((2 * i + q) * HW, HW)]).then_inc(e_es[q], 16)

            looped(sp, STEPS - 1, load_e)
            sp.wait_ge(e_esT, 2 * STEPS - 3)
            sp.dma_start(es[:, 0, :], attr16_v[:, (2 * STEPS - 2) * HW:(2 * STEPS - 1) * HW]).then_inc(e_es[0], 16)
            sp.wait_ge(e_esT, 2 * STEPS - 2)
            sp.dma_start(es[0:TAIL, 1, 0:16], attr16[P * FULL:E, :]).then_inc(e_es[1], 16)

            for c in range(ACC1):
                sp.wait_ge(settled1[c], 16 * (C1 + T // ACC1))

            def load_f(n, b):
                sp.dma_start(xin[:, b, :], rows(basetab, n)).then_inc(f_in[b], 16)
                sp.dma_start(nv[:, b:b + 1], rows(nvec, n)).then_inc(f_in[b], 16)
                for c in range(ACC1):
                    sp.dma_start(agg[:, b, c * DM:(c + 1) * DM], rows(acc1[c], n)).then_inc(f_in[b], 16)

            node_traffic(sp, load_f, f_out,
                         lambda n, b: sp.dma_start(rows(out, n), nout[:, b, 0:D]).then_inc(f_st[b], 16))
            for b in range(2):
                sp.wait_ge(f_st[b], 16 * (NT // 2))

        def edge_traffic(pool, S, table, gathered, acc, settled, clears):
            n = len(acc)
            width = acc[0].shape[1]

            def gather(j):
                plain(pool)
                pool.indirect_dma_start(gathered[:, j, :], None, table,
                                        bass.IndirectOffsetOnAxis(ap=gidx[:, j:j + 1].bitcast(u32), axis=0)
                                        ).then_inc(S["gath"][j], 16)

            def add(i, j):
                pool.wait_ge(S["out"], i * RING + j + 1)
                if j % HALF == 0:
                    pool.wait_ge(S["sidx"], 2 * i + j // HALF + 1)
                wait_adds(pool, settled[j % n], clears, i * (RING // n) + j // n)
                plain(pool)
                pool.indirect_dma_start(acc[j % n], bass.IndirectOffsetOnAxis(ap=sidx[:, j:j + 1].bitcast(u32), axis=0),
                                        sums[:, j, 0:width], None, compute_op=ALU.add).then_inc(settled[j % n], 16)

            for j in range(RING):
                gather(j)
            with pool.Fori(1, STEPS) as i:
                for j in range(RING):
                    add(i - 1, j)
                    pool.wait_ge(S["used"], (i - 1) * RING + j + 1)
                    gather(j)
            for j in range(RING):
                add(STEPS - 1, j)

        @block.gpsimd
        def _(pool):
            nc.gpsimd.memset(ident[:, :], 0.0).then_inc(w_const, 1)
            nc.gpsimd.memset(before[:, :], 1.0).then_inc(w_const, 1)
            pool.wait_ge(w_const, 2)
            nc.gpsimd.affine_select(out=ident[:, :], in_=ident[:, :], compare_op=ALU.not_equal, fill=1.0, base=0,
                                    pattern=[[-1, P]], channel_multiplier=1).then_inc(w_const, 1)
            nc.gpsimd.affine_select(out=before[:, :], in_=before[:, :], compare_op=ALU.is_gt, fill=0.0, base=0,
                                    pattern=[[-1, P]], channel_multiplier=1).then_inc(w_const, 1)
            nc.gpsimd.iota(trash_i[:, :], [[0, 1]], base=N, channel_multiplier=1).then_inc(w_const, 1)

            pool.wait_ge(w_zero, 1)
            for acc, settled, z, clears in ((acc0, settled0, Z0, C0), (acc1, settled1, Z1, C1)):
                for c, a in enumerate(acc):
                    v = a.rearrange("(p r) d -> p (r d)", p=P)
                    for k in range(clears):
                        pool.dma_start(v[:, k * z:(k + 1) * z], zs[:, 0:z]).then_inc(settled[c], 16)

            pool.wait_ge(w_ready, 1)
            for b in range(2):
                pool.wait_ge(a_st[b], 16 * (NT // 2))
            edge_traffic(pool, stage_b, prodtab, gathered0, acc0, settled0, C0)

            def prepare(h):
                for b in range(2):
                    n = 2 * h + b
                    pool.wait_ge(c_in[b], 16 * (1 + ACC0) * (h + 1))
                    wait(pool, c_xn, n - 1)
                    plain(pool)
                    nc.gpsimd.tensor_copy(xc[:, b, 0:S0], xin[:, b, 0:S0])
                    nc.gpsimd.tensor_copy(xc[:, b, S0:D].rearrange("p (k u) -> p k u", k=3),
                                          xin[:, b, S0:D].rearrange("p (u k) -> p k u", k=3))
                    nc.gpsimd.tensor_tensor(pair[:, 0, :], agg[:, b, 0:D], agg[:, b, D:2 * D], ALU.add)
                    nc.gpsimd.tensor_tensor(pair[:, 1, :], agg[:, b, 2 * D:3 * D], agg[:, b, 3 * D:4 * D],
                                            ALU.add).then_inc(c_pair, 1)
                    pool.wait_ge(c_pair, n + 1)
                    nc.gpsimd.tensor_tensor(ac[:, b, :], pair[:, 0, :], pair[:, 1, :], ALU.add).then_inc(c_prep, 1)
                    pool.wait_ge(c_prep, n + 1)
                    wait(pool, c_zT, n)
                    for k in range(3):
                        xk = xc[:, b, S0 + V0 * k:S0 + V0 * (k + 1)]
                        ak = ac[:, b, S0 + V0 * k:S0 + V0 * (k + 1)]
                        last = nc.gpsimd.tensor_tensor(zz[:, k, :, :], xk.unsqueeze(2).to_broadcast([NP, V0, V0]),
                                                       ak.unsqueeze(1).to_broadcast([NP, V0, V0]), ALU.mult)
                    last.then_inc(c_zz, 1)

            looped(pool, NT // 2, prepare)

            pool.wait_ge(w_ready, 2)
            for b in range(2):
                pool.wait_ge(d_st[b], 32 * (NT // 2))
            edge_traffic(pool, stage_e, ftab, gathered1, acc1, settled1, C1)

        def stage_keys(dve, S, i, q, key_table):
            c = slice(HALF * q, HALF * (q + 1))
            nc.vector.tensor_copy(shc[:, 16 * q:16 * (q + 1)], sh[:, bass.ds(i * (4 * RING) + 16 * q, 16)])
            nc.vector.tensor_copy(keyc[:, c], key_table[:, bass.ds(i * RING + HALF * q, HALF)]).then_inc(S["key"], 1)
            dve.wait_ge(S["key"], 2 * i + q + 1)
            nc.vector.tensor_scalar(toff[:, c], keyc[:, c], -1.0, trash[:, 0:1], ALU.mult, ALU.add)

        def match_tile(dve, S, i, q, jj):
            j = HALF * q + jj
            if jj == 0:
                dve.wait_ge(S["kT"], 2 * i + q + 1)
            kT = bank[q][:, P * jj:P * (jj + 1)]
            wait(dve, S["same"], i * RING + j)
            nc.vector.scalar_tensor_tensor(out=junk[:, :], in0=kT, scalar=keyc[:, j:j + 1], in1=before[:, :],
                                           op0=ALU.is_equal, op1=ALU.mult, accum_out=prev[:, j:j + 1])
            wait(dve, S["sum"], i * RING + j - 1)
            nc.vector.tensor_scalar(same[:, j % 2, :], kT, keyc[:, j:j + 1], None, ALU.is_equal).then_inc(S["same"], 1)

        def next_rows(i, j, S, index_table):
            nc.vector.tensor_copy(gidx[:, j:j + 1], index_table[:, bass.ds((i + 1) * RING + j, 1)]).then_inc(S["used"], 1)

        def target_rows(dve, S, i, q, settled, clears):
            n = len(settled)
            c = slice(HALF * q, HALF * (q + 1))
            dve.wait_ge(S["same"], i * RING + HALF * (q + 1))
            nc.vector.scalar_tensor_tensor(out=moved[:, c], in0=prev[:, c], scalar=0.0, in1=toff[:, c], op0=ALU.is_gt,
                                           op1=ALU.mult).then_inc(S["tmp"], 1)
            dve.wait_ge(S["tmp"], 2 * i + q + 1)
            for a in range(n):
                wait_adds(dve, settled[a], clears, (i - 1) * (RING // n) + (q + 1) * (HALF // n))
            nc.vector.tensor_tensor(sidx[:, c], moved[:, c], keyc[:, c], ALU.add).then_inc(S["sidx"], 1)

        @block.vector
        def _(dve):
            for t in (zs[:, :], W1[:, :], LU1[:, :], WN1[:, :, :], WF1[:, :, :], sh[:, FULL * 4:]):
                nc.vector.memset(t, 0.0)
            nc.vector.memset(src_i[:, FULL:], 0)
            nc.vector.memset(dst_i[:, FULL:], 0)
            nc.vector.memset(eps[:, :], EPS).then_inc(w_zero, 1)
            dve.wait_ge(w_const, 5)
            nc.vector.tensor_copy(trash[:, :], trash_i[:, :]).then_inc(w_pad, 1)
            dve.wait_ge(w_pad, 1)
            dve.wait_ge(w_in, WIN)
            for tab_f, tab_i in ((src_f, src_i), (dst_f, dst_i)):
                nc.vector.tensor_copy(tab_f[:, 0:FULL], tab_i[:, 0:FULL])
                nc.vector.tensor_copy(tab_f[:, FULL:T], trash[:, 0:1].to_broadcast([P, T - FULL])).then_inc(w_pad, 1)
            dve.wait_ge(w_pad, 3)
            nc.vector.tensor_copy(src_f[0:TAIL, FULL:FULL + 1], src_i[0:TAIL, FULL:FULL + 1])
            nc.vector.tensor_copy(dst_f[0:TAIL, FULL:FULL + 1], dst_i[0:TAIL, FULL:FULL + 1])
            for ap, f in ((W0[:, 0:64], 1 / 8), (W0[:, 64:160], F96), (W1[:, 0:96], R32), (W1[:, 96:192], F96),
                          (W1[:, 192:384], F96 * I3), (WU110[:, :, :], I3 * F5120), (LU0[:, :], 1 / 8), (LU1[:, :], R32),
                          (WN0[:, :, :], 1 / 8), (WN1[:, :, :], R32), (WF1[:, :, :], 1 / 4), (WF2[:, 0:160], 1 / 8),
                          (WF2[:, 160:192], I3 / 8), (WS[:, :], F96), (WV[:, :], F96)):
                nc.vector.tensor_scalar(ap, ap, float(f), None, ALU.mult)
            nc.vector.tensor_copy(gidx[:, :], dst_i[:, 0:RING]).then_inc(w_ready, 1)

            def rearrange_x(h):
                for b in range(2):
                    n = 2 * h + b
                    dve.wait_ge(a_in[b], 16 * (h + 1))
                    wait(dve, a_T, n - 1)
                    nc.vector.tensor_copy(xc[:, b, 0:S0], xin[:, b, 0:S0])
                    nc.vector.tensor_copy(xc[:, b, S0:D].rearrange("p (k u) -> p k u", k=3),
                                          xin[:, b, S0:D].rearrange("p (u k) -> p k u", k=3)).then_inc(a_xc, 1)

            looped(dve, NT // 2, rearrange_x)

            def edges_b(i):
                S = stage_b
                for q in range(2):
                    stage_keys(dve, S, i, q, src_f)
                    for jj in range(HALF):
                        j = HALF * q + jj
                        p2, g = parts[:, j % 2, :], gathered0[:, j, :]
                        e0, e1 = shc[:, 4 * j + 3:4 * j + 4], shc[:, 4 * j:4 * j + 3]
                        match_tile(dve, S, i, q, jj)
                        dve.wait_ge(S["gath"][j], 16 * (i + 1))
                        nc.vector.scalar_tensor_tensor(out=p2[:, 0:D], in0=g[:, D:2 * D], scalar=e0, in1=g[:, 0:D],
                                                       op0=ALU.mult, op1=ALU.add)
                        nc.vector.tensor_tensor(p2[:, D:D + 192].rearrange("p (k u) -> p k u", k=3),
                                                g[:, 2 * D:2 * D + 192].rearrange("p (k u) -> p k u", k=3),
                                                e1.unsqueeze(2).to_broadcast([P, 3, S0]), ALU.mult)
                        nc.vector.tensor_tensor(p2[:, D + 192:D + 288].rearrange("p (k u) -> p k u", k=3),
                                                g[:, DP - V0:DP].unsqueeze(1).to_broadcast([P, 3, V0]),
                                                e1.unsqueeze(2).to_broadcast([P, 3, V0]), ALU.mult
                                                ).then_inc(S["parts"], 1)
                        next_rows(i, j, S, dst_i)
                    target_rows(dve, S, i, q, settled0, C0)

            looped(dve, STEPS, edges_b)
            dve.wait_ge(stage_b["gath"][RING - 1], 16 * STEPS)
            nc.vector.tensor_copy(gidx[:, :], src_i[:, 0:RING]).then_inc(w_ready, 1)

            def tensor_product(h):
                for b in range(2):
                    n = 2 * h + b
                    dve.wait_ge(c_prep, n + 1)
                    zv = arena[0:NP, :].rearrange("p (k r w) -> p k r w", k=3, w=V0)
                    for c in range(8):
                        dve.wait_ge(c_Y, 12 * n + c + 1)
                        nc.vector.tensor_tensor(zs[0:NP, 512 * c:512 * (c + 1)].rearrange("p (v w) -> p v w", w=S0),
                                                bank[c % 3][0:NP, :].rearrange("p (v w) -> p v w", w=S0),
                                                ac[:, b, 8 * c:8 * c + 8].unsqueeze(2).to_broadcast([NP, 8, S0]),
                                                ALU.mult).then_inc(c_Yused, 1)
                    for c in range(8, 12):
                        other = (ac, ac, xc, xc)[c - 8][:, b, S0:D].rearrange("p (k u) -> p k u", k=3)
                        part = 16 * (c % 2)
                        dve.wait_ge(c_Y, 12 * n + c + 1)
                        for k in range(3):
                            last = nc.vector.tensor_tensor(
                                zv[:, k, 16 * (c - 8):16 * (c - 7), :],
                                bank[c % 3][0:NP, :].rearrange("p (v w) -> p v w", w=V0),
                                other[:, k, part:part + 16].unsqueeze(2).to_broadcast([NP, 16, V0]), ALU.mult)
                        last.then_inc(c_Yused, 1)
                    dve.wait_ge(c_Yused, 12 * n + 12)
                    nc.vector.tensor_reduce(r0[:, :], zs[0:NP, :].rearrange("p (v w) -> p w v", w=S0), AX.X, ALU.add)
                    nc.vector.tensor_reduce(r1[:, :].rearrange("p (k w) -> p k w", k=3),
                                            zv.rearrange("p k r w -> p k w r"), AX.X, ALU.add).then_inc(c_red, 1)
                    dve.wait_ge(c_R, n + 1)
                    nc.vector.scalar_tensor_tensor(out=y[:, :], in0=xc[:, b, :], scalar=2.0, in1=bank[6][0:NP, 0:D],
                                                   op0=ALU.mult, op1=ALU.add).then_inc(c_v, 1)
                    dve.wait_ge(c_red, n + 1)
                    dve.wait_ge(c_v, 4 * n + 1)
                    nc.vector.scalar_tensor_tensor(out=y[:, 0:S0], in0=r0[:, :], scalar=float(F5120), in1=y[:, 0:S0],
                                                   op0=ALU.mult, op1=ALU.add)
                    nc.vector.scalar_tensor_tensor(out=y[:, S0:D], in0=r1[:, :], scalar=float(F4096), in1=y[:, S0:D],
                                                   op0=ALU.mult, op1=ALU.add).then_inc(c_v, 1)
                    dve.wait_ge(c_v, 4 * n + 2)
                    nc.vector.bn_stats(st6[:, :], y[:, :]).then_inc(c_v, 1)
                    dve.wait_ge(c_v, 4 * n + 3)
                    plain(dve)
                    nc.vector.bn_aggr(mv[:, :], st6[:, :]).then_inc(c_var, 1)
                    dve.wait_ge(c_sd, n + 1)
                    nc.vector.reciprocal(rstd[:, :], sd[:, :]).then_inc(c_v, 1)
                    dve.wait_ge(c_v, 4 * n + 4)
                    wait(dve, c_st[b], 16 * h)
                    nc.vector.tensor_scalar(nout[:, b, 0:D], y[:, :], mv[:, 0:1], rstd[:, 0:1], ALU.subtract,
                                            ALU.mult).then_inc(c_xn, 1)

            looped(dve, NT // 2, tensor_product)

            def layer1_maps(h):
                for b in range(2):
                    n = 2 * h + b
                    dve.wait_ge(d_mm, n + 1)
                    dve.wait_ge(d_in[b], 32 * (h + 1))
                    wait(dve, d_st[b], 32 * h)
                    nc.vector.tensor_scalar(nout[:, b, 0:D], bank[2 + b][0:NP, 0:D], nv[:, b:b + 1], None, ALU.mult)
                    nc.vector.scalar_tensor_tensor(out=nout[:, b, D:2 * D], in0=bank[2 + b][0:NP, D:2 * D],
                                                   scalar=nv[:, b:b + 1], in1=xin[:, b, :], op0=ALU.mult,
                                                   op1=ALU.add).then_inc(d_out, 1)

            looped(dve, NT // 2, layer1_maps)

            nc.vector.memset(parts[:, :, DM - 1:DM], 1.0)

            def edges_e(i):
                S = stage_e
                for q in range(2):
                    stage_keys(dve, S, i, q, dst_f)
                    for jj in range(HALF):
                        j = HALF * q + jj
                        m, g, w = parts[:, j % 2, :], gathered1[:, j, :], bank[5 + j % 2]
                        s0, s1 = shc[:, 4 * j:4 * j + 1], [shc[:, 4 * j + 1 + k:4 * j + 2 + k] for k in range(3)]
                        vec = m[:, 96:384].rearrange("p (k u) -> p k u", k=3)

                        def product(o, a, s, c):
                            return nc.vector.scalar_tensor_tensor(out=o, in0=a, scalar=s, in1=c, op0=ALU.mult,
                                                                  op1=ALU.mult)

                        match_tile(dve, S, i, q, jj)
                        dve.wait_ge(S["gath"][j], 16 * (i + 1))
                        dve.wait_ge(e_w, i * RING + j + 1)
                        product(m[:, 0:S0], w[:, 0:S0], s0, g[:, 0:S0])
                        product(vec[:, :, S0:96], w[:, 128:160].unsqueeze(1).to_broadcast([P, 3, V0]), s0,
                                g[:, S0:D].rearrange("p (k u) -> p k u", k=3))
                        for k, col in enumerate((S0, DM, DM + V0)):
                            product(vec[:, k, 0:S0], w[:, S0:128], s1[k], g[:, 0:S0])
                            last = product(m[:, col:col + V0], w[:, 160:192], s1[k], g[:, S0 + V0 * k:S0 + V0 * (k + 1)])
                        last.then_inc(S["parts"], 1)
                        next_rows(i, j, S, src_i)
                    target_rows(dve, S, i, q, settled1, C1)

            looped(dve, STEPS, edges_e)

            def finish(h):
                for b in range(2):
                    n = 2 * h + b
                    dve.wait_ge(f_in[b], 16 * (2 + ACC1) * (h + 1))
                    wait(dve, f_T, n - 1)
                    nc.vector.tensor_tensor(summed[:, b, :], agg[:, b, 0:DM], agg[:, b, DM:2 * DM],
                                            ALU.add).then_inc(f_sum, 1)
                    dve.wait_ge(f_sum, n + 1)
                    nc.vector.tensor_scalar(gain[:, 0:1], summed[:, b, DM - 1:DM], 1.0, None, ALU.max).then_inc(f_v, 1)
                    dve.wait_ge(f_v, 7 * n + 1)
                    nc.vector.reciprocal(gain[:, 1:2], gain[:, 0:1]).then_inc(f_v, 1)
                    dve.wait_ge(f_v, 7 * n + 2)
                    nc.vector.tensor_tensor(gain[:, 2:3], gain[:, 1:2], nv[:, b:b + 1], ALU.mult).then_inc(f_v, 1)
                    dve.wait_ge(f_v, 7 * n + 3)
                    dve.wait_ge(f_mm, n + 1)
                    m = bank[2 + b][0:NP, :]
                    nc.vector.tensor_scalar(gain[:, 3:4], m[:, 0:1], gain[:, 2:3], gain[:, 2:3], ALU.mult,
                                            ALU.mult).then_inc(f_v, 1)
                    dve.wait_ge(f_v, 7 * n + 4)
                    nc.vector.scalar_tensor_tensor(out=y[:, :], in0=m[:, 1:D + 1], scalar=gain[:, 3:4], in1=xin[:, b, :],
                                                   op0=ALU.mult, op1=ALU.add).then_inc(f_v, 1)
                    dve.wait_ge(f_v, 7 * n + 5)
                    nc.vector.bn_stats(st6[:, :], y[:, :]).then_inc(f_v, 1)
                    dve.wait_ge(f_v, 7 * n + 6)
                    plain(dve)
                    nc.vector.bn_aggr(mv[:, :], st6[:, :]).then_inc(f_var, 1)
                    dve.wait_ge(f_sd, n + 1)
                    nc.vector.reciprocal(rstd[:, :], sd[:, :]).then_inc(f_v, 1)
                    dve.wait_ge(f_v, 7 * n + 7)
                    wait(dve, f_st[b], 16 * h)
                    nc.vector.tensor_scalar(nout[:, b, 0:S0], y[:, 0:S0], mv[:, 0:1], rstd[:, 0:1], ALU.subtract,
                                            ALU.mult)
                    nc.vector.tensor_scalar(nout[:, b, S0:D].rearrange("p (u k) -> p k u", k=3),
                                            y[:, S0:D].rearrange("p (k u) -> p k u", k=3), mv[:, 0:1], rstd[:, 0:1],
                                            ALU.subtract, ALU.mult).then_inc(f_out, 1)

            looped(dve, NT // 2, finish)

        def to_node_major(pe, src_tile, psum):
            plain(nc.tensor)
            nc.tensor.transpose(psum[0:S0, 0:NP], src_tile[:, 0:S0], ident[0:NP, 0:NP])
            return nc.tensor.transpose(psum[0:96, NP:2 * NP], src_tile[:, S0:D], ident[0:NP, 0:NP])

        def mm(o, a, c, start=True, stop=True):
            return nc.tensor.matmul(o, a, c, start=start, stop=stop)

        @block.tensor
        def _(pe):
            pe.wait_ge(w_ready, 1)

            def products(h):
                for b in range(2):
                    n = 2 * h + b
                    pe.wait_ge(a_xc, n + 1)
                    wait(pe, a_Ts, n - 1)
                    to_node_major(pe, xc[:, b, :], bank[b]).then_inc(a_T, 1)
                    pe.wait_ge(a_Ts, n + 1)
                    wait(pe, a_out, n - 1)
                    x0T, x1T = xT[0:S0, b, 0:NP], xT[0:96, b, NP:2 * NP]
                    lo, hi = bank[2 + 2 * b], bank[3 + 2 * b]
                    mm(lo[0:NP, 0:64], x0T, W0[:, 0:64])
                    mm(lo[0:NP, 64:160], x1T, W1[:, 0:96])
                    mm(lo[0:NP, 160:224], x0T, W0[:, 64:128])
                    mm(lo[0:NP, 224:512], x1T, W1[:, 96:384])
                    mm(hi[0:NP, 0:V0], x0T, W0[:, 128:160]).then_inc(a_mm, 1)

            looped(pe, NT // 2, products)

            def key_transposes(S, i, q):
                pe.wait_ge(S["key"], 2 * i + q + 1)
                for jj in range(HALF):
                    j = HALF * q + jj
                    last = nc.tensor.transpose(bank[q][:, P * jj:P * (jj + 1)], keyc[:, j:j + 1].to_broadcast([P, P]),
                                               ident[:, :])
                last.then_inc(S["kT"], 1)

            def sums_b(i):
                S = stage_b
                for q in range(2):
                    key_transposes(S, i, q)
                    for jj in range(HALF):
                        j = HALF * q + jj
                        same_j, p2, o = same[:, j % 2, :], parts[:, j % 2, :], bank[2 + j % 2]
                        pe.wait_ge(S["same"], i * RING + j + 1)
                        pe.wait_ge(S["parts"], i * RING + j + 1)
                        wait(pe, S["out"], i * RING + j - 1)
                        mm(o[:, 0:D], same_j, p2[:, 0:D], stop=False)
                        for k in range(3):
                            mm(o[:, 0:S0], same_j, p2[:, D + S0 * k:D + S0 * (k + 1)], start=False, stop=False)
                        mm(o[:, S0:D], same_j, p2[:, D + 192:D + 288], start=False).then_inc(S["sum"], 1)

            looped(pe, STEPS, sums_b)

            def tensor_product(h):
                for b in range(2):
                    n = 2 * h + b
                    pe.wait_ge(c_prep, n + 1)
                    wait(pe, c_Ts, n)
                    plain(pe)
                    nc.tensor.transpose(bank[7][0:S0, 2 * NP:3 * NP], ac[:, b, 0:S0], ident[0:NP, 0:NP])
                    to_node_major(pe, xc[:, b, :], bank[7]).then_inc(c_T, 1)
                    pe.wait_ge(c_Ts, n + 1)
                    x0T, x1T, a0T = xT[0:S0, 0, 0:NP], xT[0:96, 0, NP:2 * NP], xT[0:S0, 0, 2 * NP:3 * NP]
                    for c in range(12):
                        wait(pe, c_Yused, 12 * n + c - 2)
                        o = bank[c % 3][0:NP, :]
                        if c < 8:
                            last = mm(o, x0T, WU0[:, 512 * c:512 * (c + 1)])
                        elif c < 10:
                            last = mm(o, x0T, WU011[:, 512 * (c - 8):512 * (c - 7)])
                        else:
                            last = mm(o, a0T, WU101[:, 512 * (c - 10):512 * (c - 9)])
                        last.then_inc(c_Y, 1)
                    pe.wait_ge(c_zz, n + 1)
                    wait(pe, c_zTs, n)
                    for c in range(8):
                        o = bank[4 + c // 4][:, NP * (c % 4):NP * (c % 4 + 1)]
                        for k in range(3):
                            z = zz[:, k, :, :].rearrange("p u v -> p (u v)")
                            last = mm(o, z[:, P * c:P * (c + 1)], ident[0:NP, 0:NP], start=k == 0, stop=k == 2)
                    last.then_inc(c_zT, 1)
                    pe.wait_ge(c_zTs, n + 1)
                    wait(pe, c_xn, n)
                    o = bank[6][0:NP, :]
                    mm(o[:, 0:S0], x0T, LU0[:, :], stop=False)
                    for c in range(8):
                        mm(o[:, 0:S0], zzT[:, NP * c:NP * (c + 1)], WU110[:, c, :], start=False, stop=c == 7)
                    mm(o[:, S0:D], x1T, LU1[:, :]).then_inc(c_R, 1)

            looped(pe, NT // 2, tensor_product)

            def layer1_maps(h):
                for b in range(2):
                    n = 2 * h + b
                    pe.wait_ge(d_in[b], 32 * (h + 1))
                    wait(pe, d_Ts, n - 1)
                    to_node_major(pe, xin[:, b, :], bank[b]).then_inc(d_T, 1)
                    pe.wait_ge(d_Ts, n + 1)
                    wait(pe, d_out, n - 1)
                    x0T, x1T, o = xT[0:S0, b, 0:NP], xT[0:96, b, NP:2 * NP], bank[2 + b][0:NP, :]
                    mm(o[:, 0:64], x0T, WN0[:, 0, :])
                    mm(o[:, 64:160], x1T, WN1[:, 0, :])
                    mm(o[:, 160:224], x0T, WN0[:, 1, :])
                    mm(o[:, 224:320], x1T, WN1[:, 1, :]).then_inc(d_mm, 1)

            looped(pe, NT // 2, layer1_maps)

            def sums_e(i):
                S = stage_e

                def radial(j):
                    wait(pe, S["parts"], i * RING + j - 1)
                    half, pr = 64 * (j % 2), (j % HALF) // 2
                    mm(bank[5 + j % 2][:, 0:192], hT[half:half + 64, pr, :], WF2[half:half + 64, :]).then_inc(e_w, 1)

                for q in range(2):
                    pe.wait_ge(e_es[q], 16 * (i + 1))
                    wait(pe, e_hs, 2 * i + q)
                    plain(pe)
                    nc.tensor.transpose(bank[4][0:HW, 0:P], es[:, q, :], ident[:, :]).then_inc(e_esT, 1)
                    key_transposes(S, i, q)
                    pe.wait_ge(e_esTs, 2 * i + q + 1)
                    for pr in range(2):
                        last = mm(bank[4][:, P * (1 + pr):P * (2 + pr)], WF1[:, pr, :], esT[:, :])
                    last.then_inc(e_h, 1)
                    pe.wait_ge(e_hs, 2 * i + q + 1)
                    radial(HALF * q)
                    for jj in range(HALF):
                        j = HALF * q + jj
                        if jj + 1 < HALF:
                            radial(j + 1)
                        same_j, m, o = same[:, j % 2, :], parts[:, j % 2, :], bank[2 + j % 2]
                        pe.wait_ge(S["same"], i * RING + j + 1)
                        pe.wait_ge(S["parts"], i * RING + j + 1)
                        wait(pe, S["out"], i * RING + j - 1)
                        mm(o[:, 0:DM], same_j, m[:, 0:DM], stop=False)
                        mm(o[:, S0:96], same_j, m[:, DM:DM + V0], start=False, stop=False)
                        mm(o[:, S0:96], same_j, m[:, DM + V0:DM + 2 * V0], start=False).then_inc(S["sum"], 1)

            looped(pe, STEPS, sums_e)

            def output_maps(h):
                for b in range(2):
                    n = 2 * h + b
                    pe.wait_ge(f_sum, n + 1)
                    wait(pe, f_Ts, n - 1)
                    for c in range(4):
                        last = nc.tensor.transpose(bank[b][0:96, NP * c:NP * (c + 1)], summed[:, b, 96 * c:96 * (c + 1)],
                                                   ident[0:NP, 0:NP])
                    last.then_inc(f_T, 1)
                    pe.wait_ge(f_Ts, n + 1)
                    wait(pe, f_out, n - 1)
                    o = bank[2 + b][0:NP, :]
                    mm(o[:, 0:1 + S0], sumT[:, b, 0:NP], WS[:, :])
                    for k in range(3):
                        last = mm(o[:, 65 + V0 * k:65 + V0 * (k + 1)], sumT[:, b, NP * (k + 1):NP * (k + 2)], WV[:, :])
                    last.then_inc(f_mm, 1)

            looped(pe, NT // 2, output_maps)

        @block.scalar
        def _(act):
            def copy(o, a):
                return nc.scalar.activation(o, a, ACT.Copy)

            def products(h):
                for b in range(2):
                    n = 2 * h + b
                    act.wait_ge(a_T, n + 1)
                    wait(act, a_mm, n - 1)
                    copy(xT[0:S0, b, 0:NP], bank[b][0:S0, 0:NP])
                    copy(xT[0:96, b, NP:2 * NP], bank[b][0:96, NP:2 * NP]).then_inc(a_Ts, 1)
                    act.wait_ge(a_mm, n + 1)
                    wait(act, a_st[b], 16 * h)
                    copy(nout[:, b, 0:512], bank[2 + 2 * b][0:NP, :])
                    copy(nout[:, b, 512:DP], bank[3 + 2 * b][0:NP, 0:V0]).then_inc(a_out, 1)

            looped(act, NT // 2, products)

            def sums_out(S, i, j, width, settled, clears):
                n = len(settled)
                act.wait_ge(S["sum"], i * RING + j + 1)
                wait_adds(act, settled[j % n], clears, (i - 1) * (RING // n) + j // n + 1)
                copy(sums[:, j, 0:width], bank[2 + j % 2][:, 0:width]).then_inc(S["out"], 1)

            def sums_b(i):
                for j in range(RING):
                    sums_out(stage_b, i, j, D, settled0, C0)

            looped(act, STEPS, sums_b)

            def tensor_product(h):
                for b in range(2):
                    n = 2 * h + b
                    act.wait_ge(c_T, n + 1)
                    copy(xT[0:S0, 0, 0:NP], bank[7][0:S0, 0:NP])
                    copy(xT[0:S0, 0, 2 * NP:3 * NP], bank[7][0:S0, 2 * NP:3 * NP])
                    copy(xT[0:96, 0, NP:2 * NP], bank[7][0:96, NP:2 * NP]).then_inc(c_Ts, 1)
                    act.wait_ge(c_zT, n + 1)
                    for c in range(2):
                        last = copy(zzT[:, 4 * NP * c:4 * NP * (c + 1)], bank[4 + c][:, 0:4 * NP])
                    last.then_inc(c_zTs, 1)
                    act.wait_ge(c_var, n + 1)
                    nc.scalar.activation(sd[:, :], mv[:, 1:2], ACT.Sqrt, bias=eps[0:NP, 0:1]).then_inc(c_sd, 1)

            looped(act, NT // 2, tensor_product)

            def layer1_maps(h):
                for b in range(2):
                    n = 2 * h + b
                    act.wait_ge(d_T, n + 1)
                    wait(act, d_mm, n - 1)
                    copy(xT[0:S0, b, 0:NP], bank[b][0:S0, 0:NP])
                    copy(xT[0:96, b, NP:2 * NP], bank[b][0:96, NP:2 * NP]).then_inc(d_Ts, 1)

            looped(act, NT // 2, layer1_maps)

            def sums_e(i):
                for q in range(2):
                    act.wait_ge(e_esT, 2 * i + q + 1)
                    copy(esT[:, :], bank[4][0:HW, 0:P]).then_inc(e_esTs, 1)
                    act.wait_ge(e_h, 2 * i + q + 1)
                    wait(act, e_w, i * RING + HALF * q)
                    nc.scalar.activation(hT[:, :, :].rearrange("p a n -> p (a n)"), bank[4][:, P:3 * P],
                                         ACT.Silu).then_inc(e_hs, 1)
                    for jj in range(HALF):
                        sums_out(stage_e, i, HALF * q + jj, DM, settled1, C1)

            looped(act, STEPS, sums_e)

            def finish(h):
                for b in range(2):
                    n = 2 * h + b
                    act.wait_ge(f_T, n + 1)
                    wait(act, f_mm, n - 1)
                    copy(sumT[:, b, :], bank[b][0:96, 0:4 * NP]).then_inc(f_Ts, 1)
                    act.wait_ge(f_var, n + 1)
                    nc.scalar.activation(sd[:, :], mv[:, 1:2], ACT.Sqrt, bias=eps[0:NP, 0:1]).then_inc(f_sd, 1)

            looped(act, NT // 2, finish)


_NAMES = ["x", "src", "dst", "edge_attr_16", "edge_attr_4", "node_vec1", "L0_gnn_wm000", "L0_gnn_wm011",
          "L0_gnn_wm101", "L0_gnn_wm110", "L0_gnn_lm0", "L0_gnn_lm1", "L0_gnn_wu000", "L0_gnn_wu011", "L0_gnn_wu101",
          "L0_gnn_wu110", "L0_gnn_lu0", "L0_gnn_lu1", "L1_gnn_Wfc1", "L1_gnn_Wfc2", "L1_gnn_Wsc0", "L1_gnn_Wsc1",
          "L1_gnn_Wl1_0", "L1_gnn_Wl1_1", "L1_gnn_Wl2_s", "L1_gnn_Wl2_v", "L1_gnn_Wa"]


def kernel(**inputs):
    import numpy as _np
    import concourse.bacc as _bacc
    from concourse import mybir as _mybir
    from concourse.bass_utils import run_bass_kernel_spmd as _run

    nc = _bacc.Bacc("TRN2", target_bir_lowering=False, num_devices=1)
    arrays, args = {}, []
    for name in _NAMES:
        a = _np.ascontiguousarray(inputs[name])
        arrays[f"in_{name}_dram"] = a
        args.append(nc.dram_tensor(f"in_{name}_dram", a.shape, _mybir.dt.from_np(a.dtype), kind="ExternalInput").ap())
    out = nc.dram_tensor("out_dram", (N, D), _mybir.dt.from_np(_np.dtype("float32")), kind="ExternalOutput").ap()
    program(nc, *args, out)
    r = _run(nc, [arrays], core_ids=[0])
    return r.results[0]["out_dram"]
```

```python
import concourse.bass as bass
from concourse import mybir
from contextlib import ExitStack
import numpy as np

N, D, E = 12500, 160, 212500
S0, V0 = 64, 32
P = 128
FULL = E // P
TAIL = E - P * FULL
HALF = 4
RING = 2 * HALF
STEPS = -(-(FULL + 1) // RING)
T = STEPS * RING
NP = 125
NT = N // NP
ROWS = N + 172
RPP = ROWS // P
DP = D + D + 3 * S0 + V0
DM = 4 * 96 + 1
ACC0, ACC1 = 4, 2
Z0, Z1 = 3960, 3465
C0 = RPP * D // Z0
C1 = RPP * DM // Z1
assert C0 * Z0 == RPP * D and C1 * Z1 == RPP * DM and NT * NP == N and T * P >= E
I3, F96, F5120, F4096 = 1 / np.sqrt(3.0), 1 / np.sqrt(96.0), 1 / np.sqrt(5120.0), 1 / 64.0
R32 = 1 / np.sqrt(32.0)
EPS = 1e-5


def program(nc, x, src, dst, attr16, attr4, nvec, wm000, wm011, wm101, wm110, lm0, lm1,
            wu000, wu011, wu101, wu110, lu0, lu1, wfc1, wfc2, wsc0, wsc1, wl10, wl11, wl2s, wl2v, wa, out):
    f32, i32, u32 = mybir.dt.float32, mybir.dt.int32, mybir.dt.uint32
    ALU, ACT, AX = mybir.AluOpType, mybir.ActivationFunctionType, mybir.AxisListType
    ctx = ExitStack()
    with ctx:
        def sb(name, shape, dt=f32):
            return ctx.enter_context(nc.sbuf_tensor(name, shape, dt))

        def sem(name):
            return ctx.enter_context(nc.semaphore(name))

        def sems(name, n):
            return [sem(f"{name}{i}") for i in range(n)]

        def dram(name, shape):
            return nc.dram_tensor(name, shape, f32, kind="Internal").ap()

        prodtab = dram("prodtab", [N, DP])
        normed = dram("normed", [N, D])
        ftab = dram("ftab", [N, D])
        basetab = dram("basetab", [N, D])
        acc0 = [dram(f"acc0_{c}", [ROWS, D]) for c in range(ACC0)]
        acc1 = [dram(f"acc1_{c}", [ROWS, DM]) for c in range(ACC1)]

        ident = sb("ident", [P, P])
        before = sb("before", [P, P])
        ones = sb("ones", [P, P])
        trash = sb("trash", [P, 1])
        trash_i = sb("trash_i", [P, 1], i32)
        eps = sb("eps", [P, 1])
        W0 = sb("W0", [S0, 160])
        W1 = sb("W1", [96, 96 + 96 + 3 * S0])
        WU0 = sb("WU0", [P, 32, S0])
        WU011 = sb("WU011", [S0, V0 * V0])
        WU101 = sb("WU101", [S0, V0 * V0])
        WU110 = sb("WU110", [P, 8, S0])
        LU0 = sb("LU0", [S0, S0])
        LU1 = sb("LU1", [96, 96])
        WN0 = sb("WN0", [S0, 2, S0])
        WN1 = sb("WN1", [96, 2, 96])
        WF1 = sb("WF1", [HALF * 16, 2, P])
        WF2 = sb("WF2", [P, 192])
        WS = sb("WS", [96, 1 + S0])
        WV = sb("WV", [96, V0])

        src_i = sb("src_i", [P, T + RING], i32)
        dst_i = sb("dst_i", [P, T + RING], i32)
        src_f = sb("src_f", [P, T + RING])
        dst_f = sb("dst_f", [P, T + RING])
        sh = sb("sh", [P, (T + RING) * 4])

        xin = sb("xin", [NP, 2, D])
        xc = sb("xc", [NP, 2, D])
        xT = sb("xT", [96, 2, 3 * NP])
        nv = sb("nv", [NP, 2])
        nout = sb("nout", [NP, 2, DP])
        arena = sb("arena", [P, 3 * S0 * V0])
        zs = sb("zs", [NP, S0 * S0])
        zeros = sb("zeros", [P, Z0])
        zz = sb("zz", [NP, 3, V0, V0])
        zzT = sb("zzT", [P, 4, 4 * NP])
        agg = sb("agg", [NP, 2, 2 * DM])
        pair = sb("pair", [NP, 2, D])
        ac = sb("ac", [NP, 2, D])
        r1 = sb("r1", [NP, 96])
        y = sb("y", [NP, D])
        st6 = sb("st6", [NP, 6])
        mv = sb("mv", [NP, 2])
        sd = sb("sd", [NP, 1])
        rstd = sb("rstd", [NP, 1])
        summed = sb("summed", [NP, 2, DM])
        sumT = sb("sumT", [96, 2, 4 * NP])
        gain = sb("gain", [NP, 4])

        gathered0 = arena[:, 0:RING * DP].rearrange("p (j d) -> p j d", j=RING)
        gathered1 = arena[:, 0:RING * D].rearrange("p (j d) -> p j d", j=RING)
        gidx = sb("gidx", [P, RING], i32)
        sidx = sb("sidx", [P, RING], i32)
        keyc = sb("keyc", [P, RING])
        shc = sb("shc", [P, RING * 4])
        toff = sb("toff", [P, RING])
        prev = sb("prev", [P, RING])
        moved = sb("moved", [P, RING])
        same = sb("same", [P, 2, P])
        junk = sb("junk", [P, P])
        MID1 = 321
        PARTS = S0 + 3 * MID1
        parts = sb("parts", [P, 2, PARTS])
        sums = sb("sums", [P, RING, DM])
        es = sb("es", [P, 2, HALF * 16])
        esT = sb("esT", [HALF * 16, P])
        hT = sb("hT", [P, 2, 2, P])
        scaled = zzT[:, :, 0:4 * 96].rearrange("p j (k u) -> p j k u", k=4)

        bank = [ctx.enter_context(nc.psum_tensor(f"bank{i}", [P, 512], f32)) for i in range(8)]

        w_in = sem("w_in")
        w_const = sem("w_const")
        w_zero = sem("w_zero")
        w_pad = sem("w_pad")
        w_ready = sem("w_ready")
        w_step = sem("w_step")
        a_in, a_xc, a_T, a_Ts, a_mm, a_out, a_st = (sems("a_in", 2), sem("a_xc"), sem("a_T"), sem("a_Ts"), sem("a_mm"),
                                                    sem("a_out"), sems("a_st", 2))
        stage_b, stage_e = [dict(gath=sems(s + "_gath", RING), used=sem(s + "_used"), key=sem(s + "_key"),
                                 kT=sem(s + "_kT"), same=sem(s + "_same"), parts=sem(s + "_parts"),
                                 sum=sem(s + "_sum"), out=sem(s + "_out"), sidx=sem(s + "_sidx"), tmp=sem(s + "_tmp"))
                            for s in "be"]
        settled0 = sems("settled0_", ACC0)
        settled1 = sems("settled1_", ACC1)
        e_es, e_esT, e_esTs, e_h, e_hs, e_w, e_ws = (sems("e_es", 2), sem("e_esT"), sem("e_esTs"), sem("e_h"), sem("e_hs"),
                                                     sem("e_w"), sem("e_ws"))
        c_in, c_pair, c_prep, c_T, c_Ts, c_Y, c_Yused = (sems("c_in", 2), sem("c_pair"), sem("c_prep"),
                                                               sem("c_T"), sem("c_Ts"), sem("c_Y"), sem("c_Yused"))
        c_zT, c_zTs, c_R, c_red, c_v, c_var, c_sd, c_xn, c_st = (sem("c_zT"), sem("c_zTs"), sem("c_R"), sem("c_red"),
                                                                 sem("c_v"), sem("c_var"), sem("c_sd"), sem("c_xn"),
                                                                 sems("c_st", 2))
        c_gp, c_gd, c_M, c_zz = sem("c_gp"), sem("c_gd"), sem("c_M"), sem("c_zz")
        d_in, d_T, d_Ts, d_mm, d_out, d_st = (sems("d_in", 2), sem("d_T"), sem("d_Ts"), sem("d_mm"), sem("d_out"),
                                              sems("d_st", 2))
        f_base = sems("f_base", 2)
        f_in, f_sum, f_T, f_Ts, f_mm, f_v, f_var, f_sd, f_out, f_st = (
            sems("f_in", 2), sem("f_sum"), sem("f_T"), sem("f_Ts"), sem("f_mm"), sem("f_v"), sem("f_var"), sem("f_sd"),
            sem("f_out"), sems("f_st", 2))
        block = ctx.enter_context(nc.Block())

        def wait(eng, s, v):
            if not isinstance(v, int) or v > 0:
                eng.wait_ge(s, v)

        def wait_adds(eng, s, clears, adds):
            eng.wait_ge(s, 16 * (clears + (max(adds, 0) if isinstance(adds, int) else adds)))

        def plain(eng):
            eng.sem_inc(w_step, 1)

        def looped(eng, count, body):
            body(0)
            with eng.Fori(1, count) as i:
                body(i)

        def pipelined(eng, first, body):
            def pair_of(h):
                body(2 * h, h, 0, lambda: first(2 * h + 1, h, 1))
                if isinstance(h, int) and h == NT // 2 - 1:
                    body(2 * h + 1, h, 1, lambda: None)
                else:
                    body(2 * h + 1, h, 1, lambda: first(2 * h + 2, h + 1, 0))

            first(0, 0, 0)
            pair_of(0)
            with eng.Fori(1, NT // 2 - 1) as h:
                pair_of(h)
            pair_of(NT // 2 - 1)

        def rows(tensor, n):
            return tensor[bass.ds(n * NP, NP), :]

        def blocks3(t, c0, w):
            return [t[32 * k:32 * k + 32, c0 + w * k:c0 + w * k + w] for k in range(3)]

        WN1f = WN1[:, :, :].rearrange("p a n -> p (a n)")
        loads = [
            (W0[:, 0:64], lm0), (W0[:, 64:128], wm000.rearrange("u a w -> u (a w)")),
            (W0[:, 128:160], wm011.rearrange("u a w -> u (a w)")),
            (WU0[:, :, :], wu000.rearrange("u v w -> (u v) w").rearrange("(c p) w -> p c w", p=P)), (WU011[:, :], wu011.rearrange("u v w -> u (v w)")),
            (WU101[:, :].rearrange("v (u w) -> v u w", u=V0), wu101.rearrange("u v w -> v u w")),
            (WU110[:, :, :], wu110.rearrange("u v w -> (u v) w").rearrange("(c p) w -> p c w", p=P)),
            (LU0[:, :], lu0), (WN0[:, 0, :], wl10), (WN0[:, 1, :], wsc0),
            (WS[:, 1:65], wl2s), (WV[:, :], wl2v),
            (src_i[:, 0:FULL], src[0:P * FULL].rearrange("(p t) -> p t", p=P)),
            (dst_i[:, 0:FULL], dst[0:P * FULL].rearrange("(p t) -> p t", p=P)),
            (src_i[0:TAIL, FULL:FULL + 1], src[P * FULL:E].rearrange("(p t) -> p t", t=1)),
            (dst_i[0:TAIL, FULL:FULL + 1], dst[P * FULL:E].rearrange("(p t) -> p t", t=1)),
            (sh[:, 0:FULL * 4], attr4[0:P * FULL, :].rearrange("(p t) a -> p (t a)", p=P)),
            (sh[0:TAIL, FULL * 4:FULL * 4 + 4], attr4[P * FULL:E, :]),
            (WS[:, 0:1], wa),
        ]
        loads += [(b, lm1) for b in blocks3(W1, 0, 32)]
        loads += [(b, wm101.rearrange("u a w -> u (a w)")) for b in blocks3(W1, 96, 32)]
        loads += [(b, wm110.rearrange("u a w -> u (a w)")) for b in blocks3(W1, 192, 64)]
        loads += [(b, lu1) for b in blocks3(LU1, 0, 32)]
        loads += [(b, wl11) for b in blocks3(WN1f, 0, 32)]
        loads += [(b, wsc1) for b in blocks3(WN1f, 96, 32)]
        loads += [(WF1[16 * j:16 * j + 16, j // 2, 64 * (j % 2):64 * (j % 2) + 64], wfc1) for j in range(HALF)]
        loads += [(WF2[r:r + 64, a:b], wfc2[:, c:c + b - a]) for r in (0, 64)
                  for a, b, c in ((0, 64, 0), (64, 96, 128), (96, 160, 64), (160, 192, 160))]
        WIN = 16 * len(loads)

        attr16_v = attr16[0:P * FULL, :].rearrange("(p t) a -> p (t a)", p=P)
        HW = HALF * 16

        attr16_v = attr16[0:P * FULL, :].rearrange("(p t) a -> p (t a)", p=P)
        HW = HALF * 16

        def node_loads(sp, used, load):
            load(0, 0)
            load(1, 1)
            with sp.Fori(0, NT // 2 - 1) as h:
                for b in range(2):
                    sp.wait_ge(used, 2 * h + b + 1)
                    load(2 * h + b + 2, b)

        def node_stores(eng, ready, store):
            with eng.Fori(0, NT // 2) as h:
                for b in range(2):
                    eng.wait_ge(ready, 2 * h + b + 1)
                    plain(eng)
                    store(2 * h + b, b)

        @block.sync
        def _(sp):
            sp.wait_ge(w_zero, 1)
            for to, frm in loads:
                sp.dma_start(to, frm).then_inc(w_in, 16)

            node_loads(sp, a_xc, lambda n, b: sp.dma_start(xin[:, b, :], rows(x, n)).then_inc(a_in[b], 16))

            for c in range(ACC0):
                sp.wait_ge(settled0[c], 16 * (C0 + T // ACC0))

            def load_c(n, b):
                sp.dma_start(xin[:, b, :], rows(x, n)).then_inc(c_in[b], 16)
                for c in range(ACC0):
                    sp.dma_start(agg[:, b, c * D:(c + 1) * D], rows(acc0[c], n)).then_inc(c_in[b], 16)

            node_loads(sp, c_prep, load_c)

            for b in range(2):
                sp.wait_ge(c_st[b], 16 * (NT // 2))

            def load_d(n, b):
                sp.dma_start(xin[:, b, :], rows(normed, n)).then_inc(d_in[b], 16)
                sp.dma_start(nv[:, b:b + 1], rows(nvec, n)).then_inc(d_in[b], 16)

            node_loads(sp, d_out, load_d)

            def load_e(i):
                for q in range(2):
                    wait(sp, e_esT, 2 * i + q - 1)
                    sp.dma_start(es[:, q, :], attr16_v[:, bass.ds((2 * i + q) * HW, HW)]).then_inc(e_es[q], 16)

            looped(sp, STEPS - 1, load_e)
            sp.wait_ge(e_esT, 2 * STEPS - 3)
            sp.dma_start(es[:, 0, :], attr16_v[:, (2 * STEPS - 2) * HW:(2 * STEPS - 1) * HW]).then_inc(e_es[0], 16)
            sp.wait_ge(e_esT, 2 * STEPS - 2)
            sp.dma_start(es[0:TAIL, 1, 0:16], attr16[P * FULL:E, :]).then_inc(e_es[1], 16)
            sp.wait_ge(e_esT, 2 * STEPS - 1)
            sp.dma_start(es[:, 0, :], attr16_v[:, 0:HW]).then_inc(e_es[0], 16)

            for c in range(ACC1):
                sp.wait_ge(settled1[c], 16 * (C1 + T // ACC1))

            def load_sums(n, b):
                for c in range(ACC1):
                    sp.dma_start(agg[:, b, c * DM:(c + 1) * DM], rows(acc1[c], n)).then_inc(f_in[b], 16)

            def load_base(n, b):
                sp.dma_start(xin[:, b, :], rows(basetab, n)).then_inc(f_base[b], 16)
                sp.dma_start(nv[:, b:b + 1], rows(nvec, n)).then_inc(f_base[b], 16)

            for b in range(2):
                load_sums(b, b)
                load_base(b, b)
            with sp.Fori(0, NT // 2 - 1) as h:
                for b in range(2):
                    sp.wait_ge(f_sum, 2 * h + b + 1)
                    load_sums(2 * h + b + 2, b)
                    sp.wait_ge(f_out, 2 * h + b + 1)
                    load_base(2 * h + b + 2, b)
            for b in range(2):
                sp.wait_ge(f_st[b], 16 * (NT // 2))

        def scalar_products(eng, nc_eng, n, b, g):
            wait(eng, c_zT, 10 * (n - 1) + g + 1)
            return nc_eng.tensor_tensor(zs[0:NP, 512 * g:512 * (g + 1)].rearrange("p (u v) -> p u v", v=S0),
                                        xc[:, b, 8 * g:8 * g + 8].unsqueeze(2).to_broadcast([NP, 8, S0]),
                                        ac[:, b, 0:S0].unsqueeze(1).to_broadcast([NP, 8, S0]), ALU.mult)

        def clear(pool, acc, settled, z, clears):
            for c, a in enumerate(acc):
                v = a.rearrange("(p r) d -> p (r d)", p=P)
                for k in range(clears):
                    pool.dma_start(v[:, k * z:(k + 1) * z], zeros[:, 0:z]).then_inc(settled[c], 16)

        def edge_traffic(pool, S, table, gathered, acc, settled, clears):
            n = len(acc)
            width = acc[0].shape[1]

            def gather(j):
                plain(pool)
                pool.indirect_dma_start(gathered[:, j, :], None, table,
                                        bass.IndirectOffsetOnAxis(ap=gidx[:, j:j + 1].bitcast(u32), axis=0)
                                        ).then_inc(S["gath"][j], 16)

            def add(i, j):
                pool.wait_ge(S["out"], i * RING + j + 1)
                if j % HALF == 0:
                    pool.wait_ge(S["sidx"], 2 * i + j // HALF + 1)
                wait_adds(pool, settled[j % n], clears, i * (RING // n) + j // n)
                plain(pool)
                pool.indirect_dma_start(acc[j % n], bass.IndirectOffsetOnAxis(ap=sidx[:, j:j + 1].bitcast(u32), axis=0),
                                        sums[:, j, 0:width], None, compute_op=ALU.add).then_inc(settled[j % n], 16)

            for j in range(RING):
                gather(j)
            with pool.Fori(1, STEPS) as i:
                for j in range(RING):
                    add(i - 1, j)
                    pool.wait_ge(S["used"], (i - 1) * RING + j + 1)
                    gather(j)
            for j in range(RING):
                add(STEPS - 1, j)

        @block.gpsimd
        def _(pool):
            nc.gpsimd.memset(ident[:, :], 0.0).then_inc(w_const, 1)
            nc.gpsimd.memset(before[:, :], 1.0).then_inc(w_const, 1)
            pool.wait_ge(w_const, 2)
            nc.gpsimd.affine_select(out=ident[:, :], in_=ident[:, :], compare_op=ALU.not_equal, fill=1.0, base=0,
                                    pattern=[[-1, P]], channel_multiplier=1).then_inc(w_const, 1)
            nc.gpsimd.affine_select(out=before[:, :], in_=before[:, :], compare_op=ALU.is_gt, fill=0.0, base=0,
                                    pattern=[[-1, P]], channel_multiplier=1).then_inc(w_const, 1)
            nc.gpsimd.iota(trash_i[:, :], [[0, 1]], base=N, channel_multiplier=1).then_inc(w_const, 1)

            pool.wait_ge(w_zero, 1)
            pool.wait_ge(w_in, WIN)
            clear(pool, acc0, settled0, Z0, C0)

            node_stores(pool, a_out, lambda n, b: pool.dma_start(rows(prodtab, n), nout[:, b, :]).then_inc(a_st[b], 16))

            pool.wait_ge(w_ready, 1)
            for b in range(2):
                pool.wait_ge(a_st[b], 16 * (NT // 2))
            edge_traffic(pool, stage_b, prodtab, gathered0, acc0, settled0, C0)
            clear(pool, acc1, settled1, Z1, C1)

            def prepare(h):
                for b in range(2):
                    n = 2 * h + b
                    pool.wait_ge(c_in[b], 16 * (1 + ACC0) * (h + 1))
                    wait(pool, c_xn, n - 1)
                    plain(pool)
                    nc.gpsimd.tensor_copy(xc[:, b, 0:S0], xin[:, b, 0:S0])
                    nc.gpsimd.tensor_copy(xc[:, b, S0:D].rearrange("p (k u) -> p k u", k=3),
                                          xin[:, b, S0:D].rearrange("p (u k) -> p k u", k=3))
                    nc.gpsimd.tensor_tensor(pair[:, 0, :], agg[:, b, 0:D], agg[:, b, D:2 * D], ALU.add)
                    nc.gpsimd.tensor_tensor(pair[:, 1, :], agg[:, b, 2 * D:3 * D], agg[:, b, 3 * D:4 * D],
                                            ALU.add).then_inc(c_pair, 1)
                    pool.wait_ge(c_pair, n + 1)
                    nc.gpsimd.tensor_tensor(ac[:, b, :], pair[:, 0, :], pair[:, 1, :], ALU.add).then_inc(c_prep, 1)
                    pool.wait_ge(c_prep, n + 1)
                    for g in range(4):
                        scalar_products(pool, nc.gpsimd, n, b, g).then_inc(c_gp, 1)
                    wait(pool, c_zT, 10 * n)
                    for k in range(3):
                        xk = xc[:, b, S0 + V0 * k:S0 + V0 * (k + 1)]
                        ak = ac[:, b, S0 + V0 * k:S0 + V0 * (k + 1)]
                        last = nc.gpsimd.tensor_tensor(zz[:, k, :, :], xk.unsqueeze(2).to_broadcast([NP, V0, V0]),
                                                       ak.unsqueeze(1).to_broadcast([NP, V0, V0]), ALU.mult)
                    last.then_inc(c_zz, 1)
                    pool.wait_ge(c_zz, 2 * n + 1)
                    nc.gpsimd.tensor_tensor(zz[:, 0, :, :], zz[:, 0, :, :], zz[:, 1, :, :], ALU.add).then_inc(c_zz, 1)
                    pool.wait_ge(c_zz, 2 * n + 2)
                    nc.gpsimd.tensor_tensor(zz[:, 0, :, :], zz[:, 0, :, :], zz[:, 2, :, :], ALU.add).then_inc(c_gp, 1)

            looped(pool, NT // 2, prepare)

            def store_d(n, b):
                pool.dma_start(rows(ftab, n), nout[:, b, 0:D]).then_inc(d_st[b], 16)
                pool.dma_start(rows(basetab, n), nout[:, b, D:2 * D]).then_inc(d_st[b], 16)

            node_stores(pool, d_out, store_d)

            pool.wait_ge(w_ready, 2)
            for b in range(2):
                pool.wait_ge(d_st[b], 32 * (NT // 2))
            edge_traffic(pool, stage_e, ftab, gathered1, acc1, settled1, C1)

            node_stores(pool, f_out, lambda n, b: pool.dma_start(rows(out, n), nout[:, b, 0:D]).then_inc(f_st[b], 16))

        def next_half(i, q):
            return (i, 1) if q == 0 else (i + 1, 0)

        def two_on(i, j):
            return (i, j + 2) if j + 2 < RING else (i + 1, j + 2 - RING)

        def stage_keys(dve, S, i, q, key_table):
            c = slice(HALF * q, HALF * (q + 1))
            wait(dve, S["sidx"], 2 * i + q - 1)
            nc.vector.tensor_copy(shc[:, 16 * q:16 * (q + 1)], sh[:, bass.ds(i * (4 * RING) + 16 * q, 16)])
            nc.vector.tensor_copy(keyc[:, c], key_table[:, bass.ds(i * RING + HALF * q, HALF)]).then_inc(S["key"], 1)
            dve.wait_ge(S["key"], 2 * i + q + 1)
            nc.vector.tensor_scalar(toff[:, c], keyc[:, c], -1.0, trash[:, 0:1], ALU.mult, ALU.add)

        def match_tile(dve, S, i, q, jj):
            j = HALF * q + jj
            if jj == 0:
                dve.wait_ge(S["kT"], 2 * i + q + 1)
            kT = bank[q][:, P * jj:P * (jj + 1)]
            wait(dve, S["same"], i * RING + j)
            nc.vector.scalar_tensor_tensor(out=junk[:, :], in0=kT, scalar=keyc[:, j:j + 1], in1=before[:, :],
                                           op0=ALU.is_equal, op1=ALU.mult, accum_out=prev[:, j:j + 1])
            wait(dve, S["sum"], i * RING + j - 1)
            nc.vector.tensor_scalar(same[:, j % 2, :], kT, keyc[:, j:j + 1], None, ALU.is_equal).then_inc(S["same"], 1)

        def next_rows(i, j, S, index_table):
            nc.vector.tensor_copy(gidx[:, j:j + 1], index_table[:, bass.ds((i + 1) * RING + j, 1)]).then_inc(S["used"], 1)

        def target_rows(dve, S, i, q, settled, clears):
            n = len(settled)
            c = slice(HALF * q, HALF * (q + 1))
            dve.wait_ge(S["same"], i * RING + HALF * (q + 1))
            nc.vector.scalar_tensor_tensor(out=moved[:, c], in0=prev[:, c], scalar=0.0, in1=toff[:, c], op0=ALU.is_gt,
                                           op1=ALU.mult).then_inc(S["tmp"], 1)
            dve.wait_ge(S["tmp"], 2 * i + q + 1)
            for a in range(n):
                wait_adds(dve, settled[a], clears, (i - 1) * (RING // n) + (q + 1) * (HALF // n))
            nc.vector.tensor_tensor(sidx[:, c], moved[:, c], keyc[:, c], ALU.add).then_inc(S["sidx"], 1)

        @block.vector
        def _(dve):
            for t in (zeros[:, :], W1[:, :], LU1[:, :], WN1[:, :, :], WF1[:, :, :], sh[:, FULL * 4:]):
                nc.vector.memset(t, 0.0)
            nc.vector.memset(src_i[:, FULL:], 0)
            nc.vector.memset(dst_i[:, FULL:], 0)
            nc.vector.memset(eps[:, :], EPS).then_inc(w_zero, 1)
            dve.wait_ge(w_const, 5)
            nc.vector.tensor_copy(trash[:, :], trash_i[:, :]).then_inc(w_pad, 1)
            dve.wait_ge(w_pad, 1)
            dve.wait_ge(w_in, WIN)
            for tab_f, tab_i in ((src_f, src_i), (dst_f, dst_i)):
                nc.vector.tensor_copy(tab_f[:, 0:FULL], tab_i[:, 0:FULL])
                nc.vector.tensor_copy(tab_f[:, FULL:], trash[:, 0:1].to_broadcast([P, T + RING - FULL])).then_inc(w_pad, 1)
            dve.wait_ge(w_pad, 3)
            nc.vector.tensor_copy(src_f[0:TAIL, FULL:FULL + 1], src_i[0:TAIL, FULL:FULL + 1])
            nc.vector.tensor_copy(dst_f[0:TAIL, FULL:FULL + 1], dst_i[0:TAIL, FULL:FULL + 1])
            for ap, f in ((W0[:, 0:64], 1 / 8), (W0[:, 64:160], F96), (W1[:, 0:96], R32), (W1[:, 96:192], F96),
                          (W1[:, 192:384], F96 * I3), (WU110[:, :, :], I3 * F5120), (WU0[:, :, :], F5120), (LU0[:, :], 1 / 8), (LU1[:, :], R32),
                          (WN0[:, :, :], 1 / 8), (WN1[:, :, :], R32), (WF1[:, :, :], 1 / 4), (WF2[:, 0:160], 1 / 8),
                          (WF2[:, 160:192], I3 / 8), (WS[:, :], F96), (WV[:, :], F96)):
                nc.vector.tensor_scalar(ap, ap, float(f), None, ALU.mult)
            nc.vector.tensor_copy(gidx[:, :], dst_i[:, 0:RING]).then_inc(w_ready, 1)

            def rearrange_x(h):
                for b in range(2):
                    n = 2 * h + b
                    dve.wait_ge(a_in[b], 16 * (h + 1))
                    wait(dve, a_T, n - 1)
                    nc.vector.tensor_copy(xc[:, b, 0:S0], xin[:, b, 0:S0])
                    nc.vector.tensor_copy(xc[:, b, S0:D].rearrange("p (k u) -> p k u", k=3),
                                          xin[:, b, S0:D].rearrange("p (u k) -> p k u", k=3)).then_inc(a_xc, 1)

            looped(dve, NT // 2, rearrange_x)

            def edges_b(i):
                S = stage_b
                for q in range(2):
                    for jj in range(HALF):
                        j = HALF * q + jj
                        p2, g = parts[:, j % 2, :], gathered0[:, j, :]
                        e0, e1 = shc[:, 4 * j + 3:4 * j + 4], shc[:, 4 * j:4 * j + 3]
                        match_tile(dve, S, i, q, jj)
                        dve.wait_ge(S["gath"][j], 16 * (i + 1))
                        nc.vector.scalar_tensor_tensor(out=p2[:, 0:D], in0=g[:, D:2 * D], scalar=e0, in1=g[:, 0:D],
                                                       op0=ALU.mult, op1=ALU.add)
                        nc.vector.tensor_tensor(p2[:, D:D + 192].rearrange("p (k u) -> p k u", k=3),
                                                g[:, 2 * D:2 * D + 192].rearrange("p (k u) -> p k u", k=3),
                                                e1.unsqueeze(2).to_broadcast([P, 3, S0]), ALU.mult)
                        nc.vector.tensor_tensor(p2[:, D + 192:D + 288].rearrange("p (k u) -> p k u", k=3),
                                                g[:, DP - V0:DP].unsqueeze(1).to_broadcast([P, 3, V0]),
                                                e1.unsqueeze(2).to_broadcast([P, 3, V0]), ALU.mult
                                                ).then_inc(S["parts"], 1)
                        next_rows(i, j, S, dst_i)
                        if jj == 0:
                            stage_keys(dve, S, *next_half(i, q), src_f)
                    target_rows(dve, S, i, q, settled0, C0)

            stage_keys(dve, stage_b, 0, 0, src_f)
            looped(dve, STEPS, edges_b)
            dve.wait_ge(stage_b["kT"], 2 * STEPS + 1)
            nc.vector.tensor_copy(gidx[:, :], src_i[:, 0:RING]).then_inc(w_ready, 1)

            def tensor_product(h):
                for b in range(2):
                    n = 2 * h + b
                    dve.wait_ge(c_prep, n + 1)
                    for g in range(4, 8):
                        scalar_products(dve, nc.vector, n, b, g).then_inc(c_gd, 1)
                    zv = arena[0:NP, :].rearrange("p (k r w) -> p k r w", k=3, w=V0)
                    wait(dve, c_red, n)
                    for c in range(4):
                        other = (ac, ac, xc, xc)[c][:, b, S0:D].rearrange("p (k u) -> p k u", k=3)
                        part = 16 * (c % 2)
                        dve.wait_ge(c_Y, 4 * n + c + 1)
                        for k in range(3):
                            last = nc.vector.tensor_tensor(
                                zv[:, k, 16 * c:16 * (c + 1), :], bank[c][0:NP, :].rearrange("p (v w) -> p v w", w=V0),
                                other[:, k, part:part + 16].unsqueeze(2).to_broadcast([NP, 16, V0]), ALU.mult)
                        last.then_inc(c_Yused, 1)
                    dve.wait_ge(c_Yused, 4 * n + 4)
                    nc.vector.tensor_reduce(r1[:, :].rearrange("p (k w) -> p k w", k=3),
                                            zv.rearrange("p k r w -> p k w r"), AX.X, ALU.add).then_inc(c_red, 1)
                    dve.wait_ge(c_R, n + 1)
                    wait(dve, c_xn, n)
                    nc.vector.scalar_tensor_tensor(out=y[:, :], in0=xc[:, b, :], scalar=2.0, in1=bank[6][0:NP, 0:D],
                                                   op0=ALU.mult, op1=ALU.add).then_inc(c_v, 1)
                    dve.wait_ge(c_red, n + 1)
                    dve.wait_ge(c_v, 4 * n + 1)
                    nc.vector.scalar_tensor_tensor(out=y[:, S0:D], in0=r1[:, :], scalar=float(F4096), in1=y[:, S0:D],
                                                   op0=ALU.mult, op1=ALU.add).then_inc(c_v, 1)
                    dve.wait_ge(c_v, 4 * n + 2)
                    nc.vector.bn_stats(st6[:, :], y[:, :]).then_inc(c_v, 1)
                    dve.wait_ge(c_v, 4 * n + 3)
                    plain(dve)
                    nc.vector.bn_aggr(mv[:, :], st6[:, :]).then_inc(c_var, 1)
                    dve.wait_ge(c_sd, n + 1)
                    nc.vector.reciprocal(rstd[:, :], sd[:, :]).then_inc(c_v, 1)
                    dve.wait_ge(c_v, 4 * n + 4)
                    wait(dve, c_st[b], 16 * h)
                    nc.vector.tensor_scalar(nout[:, b, 0:D], y[:, :], mv[:, 0:1], rstd[:, 0:1], ALU.subtract,
                                            ALU.mult).then_inc(c_xn, 1)

            looped(dve, NT // 2, tensor_product)

            def layer1_maps(h):
                for b in range(2):
                    n = 2 * h + b
                    dve.wait_ge(d_mm, n + 1)
                    dve.wait_ge(d_in[b], 32 * (h + 1))
                    wait(dve, d_st[b], 32 * h)
                    nc.vector.tensor_scalar(nout[:, b, 0:D], bank[2 + b][0:NP, 0:D], nv[:, b:b + 1], None, ALU.mult)
                    nc.vector.scalar_tensor_tensor(out=nout[:, b, D:2 * D], in0=bank[2 + b][0:NP, D:2 * D],
                                                   scalar=nv[:, b:b + 1], in1=xin[:, b, :], op0=ALU.mult,
                                                   op1=ALU.add).then_inc(d_out, 1)

            looped(dve, NT // 2, layer1_maps)

            nc.vector.memset(parts[:, :, DM - 1:DM], 1.0)

            def edges_e(i):
                S = stage_e
                for q in range(2):
                    for jj in range(HALF):
                        j = HALF * q + jj
                        m, g, w = parts[:, j % 2, :], gathered1[:, j, :], scaled[:, j % 4, :, :]
                        vec = m[:, 96:384].rearrange("p (k u) -> p k u", k=3)
                        gv = g[:, S0:D].rearrange("p (k u) -> p k u", k=3)
                        match_tile(dve, S, i, q, jj)
                        dve.wait_ge(S["gath"][j], 16 * (i + 1))
                        dve.wait_ge(e_ws, i * RING + j + 1)
                        nc.vector.tensor_tensor(m[:, 0:4 * 96].rearrange("p (k u) -> p k u", k=4)[:, :, 0:S0],
                                                w[:, :, 0:S0], g[:, 0:S0].unsqueeze(1).to_broadcast([P, 4, S0]),
                                                ALU.mult)
                        nc.vector.tensor_tensor(vec[:, :, S0:96], w[:, 0:1, S0:96].to_broadcast([P, 3, V0]), gv,
                                                ALU.mult)
                        nc.vector.tensor_tensor(m[:, S0:S0 + 3 * MID1].rearrange("p (k u) -> p k u", k=3)[:, :, 0:V0],
                                                w[:, 1:4, S0:96], gv, ALU.mult).then_inc(S["parts"], 1)
                        next_rows(i, j, S, src_i)
                        if jj == 0:
                            stage_keys(dve, S, *next_half(i, q), dst_f)
                    target_rows(dve, S, i, q, settled1, C1)

            stage_keys(dve, stage_e, 0, 0, dst_f)
            looped(dve, STEPS, edges_e)

            def sum_accumulators(n, h, b):
                dve.wait_ge(f_in[b], 16 * ACC1 * (h + 1))
                wait(dve, f_T, n - 1)
                nc.vector.tensor_tensor(summed[:, b, :], agg[:, b, 0:DM], agg[:, b, DM:2 * DM], ALU.add).then_inc(f_sum, 1)

            def finish(n, h, b, following):
                    following()
                    dve.wait_ge(f_sum, n + 1)
                    wait(dve, f_out, n)
                    dve.wait_ge(f_base[b], 32 * (h + 1))
                    nc.vector.tensor_scalar(gain[:, 0:1], summed[:, b, DM - 1:DM], 1.0, None, ALU.max).then_inc(f_v, 1)
                    dve.wait_ge(f_v, 7 * n + 1)
                    nc.vector.reciprocal(gain[:, 1:2], gain[:, 0:1]).then_inc(f_v, 1)
                    dve.wait_ge(f_v, 7 * n + 2)
                    nc.vector.tensor_tensor(gain[:, 2:3], gain[:, 1:2], nv[:, b:b + 1], ALU.mult).then_inc(f_v, 1)
                    dve.wait_ge(f_v, 7 * n + 3)
                    dve.wait_ge(f_mm, n + 1)
                    m = bank[2 + b][0:NP, :]
                    nc.vector.tensor_scalar(gain[:, 3:4], m[:, 0:1], gain[:, 2:3], gain[:, 2:3], ALU.mult,
                                            ALU.mult).then_inc(f_v, 1)
                    dve.wait_ge(f_v, 7 * n + 4)
                    nc.vector.scalar_tensor_tensor(out=y[:, :], in0=m[:, 1:D + 1], scalar=gain[:, 3:4], in1=xin[:, b, :],
                                                   op0=ALU.mult, op1=ALU.add).then_inc(f_v, 1)
                    dve.wait_ge(f_v, 7 * n + 5)
                    nc.vector.bn_stats(st6[:, :], y[:, :]).then_inc(f_v, 1)
                    dve.wait_ge(f_v, 7 * n + 6)
                    plain(dve)
                    nc.vector.bn_aggr(mv[:, :], st6[:, :]).then_inc(f_var, 1)
                    dve.wait_ge(f_sd, n + 1)
                    nc.vector.reciprocal(rstd[:, :], sd[:, :]).then_inc(f_v, 1)
                    dve.wait_ge(f_v, 7 * n + 7)
                    wait(dve, f_st[b], 16 * h)
                    nc.vector.tensor_scalar(nout[:, b, 0:S0], y[:, 0:S0], mv[:, 0:1], rstd[:, 0:1], ALU.subtract,
                                            ALU.mult)
                    nc.vector.tensor_scalar(nout[:, b, S0:D].rearrange("p (u k) -> p k u", k=3),
                                            y[:, S0:D].rearrange("p (k u) -> p k u", k=3), mv[:, 0:1], rstd[:, 0:1],
                                            ALU.subtract, ALU.mult).then_inc(f_out, 1)

            pipelined(dve, sum_accumulators, finish)

        def to_node_major(pe, src_tile, psum):
            plain(nc.tensor)
            nc.tensor.transpose(psum[0:S0, 0:NP], src_tile[:, 0:S0], ident[0:NP, 0:NP])
            return nc.tensor.transpose(psum[0:96, NP:2 * NP], src_tile[:, S0:D], ident[0:NP, 0:NP])

        def mm(o, a, c, start=True, stop=True):
            return nc.tensor.matmul(o, a, c, start=start, stop=stop)

        @block.tensor
        def _(pe):
            pe.wait_ge(w_ready, 1)

            def transpose_a(n, h, b):
                pe.wait_ge(a_xc, n + 1)
                wait(pe, a_Ts, n - 1)
                to_node_major(pe, xc[:, b, :], bank[b]).then_inc(a_T, 1)

            def products(n, h, b, following):
                following()
                pe.wait_ge(a_Ts, n + 1)
                wait(pe, a_out, n - 1)
                x0T, x1T = xT[0:S0, b, 0:NP], xT[0:96, b, NP:2 * NP]
                lo, hi = bank[2 + 2 * b], bank[3 + 2 * b]
                mm(lo[0:NP, 0:64], x0T, W0[:, 0:64])
                mm(lo[0:NP, 64:160], x1T, W1[:, 0:96])
                mm(lo[0:NP, 160:224], x0T, W0[:, 64:128])
                mm(lo[0:NP, 224:512], x1T, W1[:, 96:384])
                mm(hi[0:NP, 0:V0], x0T, W0[:, 128:160]).then_inc(a_mm, 1)

            pipelined(pe, transpose_a, products)

            def key_transposes(S, i, q):
                pe.wait_ge(S["key"], 2 * i + q + 1)
                for jj in range(HALF):
                    j = HALF * q + jj
                    last = nc.tensor.transpose(bank[q][:, P * jj:P * (jj + 1)], keyc[:, j:j + 1].to_broadcast([P, P]),
                                               ident[:, :])
                last.then_inc(S["kT"], 1)

            def sums_b(i):
                S = stage_b
                for q in range(2):
                    for jj in range(HALF):
                        j = HALF * q + jj
                        same_j, p2, o = same[:, j % 2, :], parts[:, j % 2, :], bank[2 + j % 2]
                        pe.wait_ge(S["same"], i * RING + j + 1)
                        pe.wait_ge(S["parts"], i * RING + j + 1)
                        wait(pe, S["out"], i * RING + j - 1)
                        mm(o[:, 0:D], same_j, p2[:, 0:D], stop=False)
                        for k in range(3):
                            mm(o[:, 0:S0], same_j, p2[:, D + S0 * k:D + S0 * (k + 1)], start=False, stop=False)
                        mm(o[:, S0:D], same_j, p2[:, D + 192:D + 288], start=False).then_inc(S["sum"], 1)
                        if jj == 1:
                            key_transposes(S, *next_half(i, q))

            key_transposes(stage_b, 0, 0)
            looped(pe, STEPS, sums_b)

            def transpose_c(n, h, b):
                pe.wait_ge(c_prep, n + 1)
                wait(pe, c_Ts, n)
                plain(pe)
                nc.tensor.transpose(bank[7][0:S0, 2 * NP:3 * NP], ac[:, b, 0:S0], ident[0:NP, 0:NP])
                to_node_major(pe, xc[:, b, :], bank[7]).then_inc(c_T, 1)

            def transpose_group(n, g):
                if g < 4:
                    pe.wait_ge(c_gp, 5 * n + g + 1)
                elif g < 8:
                    pe.wait_ge(c_gd, 4 * n + g - 3)
                else:
                    pe.wait_ge(c_gp, 5 * n + 5)
                wait(pe, c_zTs, 10 * n + g - 1)
                of = zs[0:NP, 512 * g:512 * (g + 1)] if g < 8 else \
                    zz[:, 0, :, :].rearrange("p u v -> p (u v)")[:, 512 * (g - 8):512 * (g - 7)]
                for c in range(4):
                    last = nc.tensor.transpose(bank[4 + g % 2][:, NP * c:NP * (c + 1)], of[:, P * c:P * (c + 1)],
                                               ident[0:NP, 0:NP])
                last.then_inc(c_zT, 1)

            def contract_group(n, g):
                pe.wait_ge(c_zTs, 10 * n + g + 1)
                if g == 0:
                    wait(pe, c_xn, n)
                for c in range(4):
                    weights = WU0[:, 4 * g + c, :] if g < 8 else WU110[:, 4 * (g - 8) + c, :]
                    last = mm(bank[6][0:NP, 0:S0], zzT[:, g % 4, NP * c:NP * (c + 1)], weights,
                              start=g == 0 and c == 0, stop=False)
                last.then_inc(c_M, 1)

            def tensor_product(n, h, b, following):
                pe.wait_ge(c_Ts, n + 1)
                x0T, x1T, a0T = xT[0:S0, b, 0:NP], xT[0:96, b, NP:2 * NP], xT[0:S0, b, 2 * NP:3 * NP]
                for c in range(4):
                    wait(pe, c_Yused, 4 * (n - 1) + c + 1)
                    w = WU011 if c < 2 else WU101
                    mm(bank[c][0:NP, :], x0T if c < 2 else a0T, w[:, 512 * (c % 2):512 * (c % 2 + 1)]).then_inc(c_Y, 1)
                for g in range(11):
                    if g < 10:
                        transpose_group(n, g)
                    if g == 7:
                        following()
                    if g > 0:
                        contract_group(n, g - 1)
                mm(bank[6][0:NP, 0:S0], x0T, LU0[:, :], start=False)
                mm(bank[6][0:NP, S0:D], x1T, LU1[:, :]).then_inc(c_R, 1)

            pipelined(pe, transpose_c, tensor_product)

            def transpose_d(n, h, b):
                pe.wait_ge(d_in[b], 32 * (h + 1))
                wait(pe, d_Ts, n - 1)
                to_node_major(pe, xin[:, b, :], bank[b]).then_inc(d_T, 1)

            def map_tile(n, h, b):
                transpose_d(n, h, b)
                pe.wait_ge(d_Ts, n + 1)
                wait(pe, d_out, n - 1)
                x0T, x1T, o = xT[0:S0, b, 0:NP], xT[0:96, b, NP:2 * NP], bank[2 + b][0:NP, :]
                mm(o[:, 0:64], x0T, WN0[:, 0, :])
                mm(o[:, 64:160], x1T, WN1[:, 0, :])
                mm(o[:, 160:224], x0T, WN0[:, 1, :])
                mm(o[:, 224:320], x1T, WN1[:, 1, :]).then_inc(d_mm, 1)

            def layer1_maps(h):
                for b in range(2):
                    map_tile(2 * h + b, h, b)

            looped(pe, NT // 2, layer1_maps)

            def edge_scalars(i, q):
                pe.wait_ge(e_es[q], 16 * (i + 1))
                wait(pe, e_esTs, 2 * i + q)
                plain(pe)
                nc.tensor.transpose(bank[4][0:HW, 0:P], es[:, q, :], ident[:, :]).then_inc(e_esT, 1)

            def hidden(i, q):
                pe.wait_ge(e_esTs, 2 * i + q + 1)
                wait(pe, e_hs, 2 * i + q)
                for pr in range(2):
                    last = mm(bank[4][:, P * (1 + pr):P * (2 + pr)], WF1[:, pr, :], esT[:, :])
                last.then_inc(e_h, 1)

            def radial(i, j):
                if j % HALF == 0:
                    pe.wait_ge(e_hs, 2 * i + j // HALF + 1)
                wait(pe, e_ws, i * RING + j - 1)
                half = 64 * (j % 2)
                mm(bank[5 + j % 2][:, 0:192], hT[half:half + 64, j // HALF, (j % HALF) // 2, :],
                   WF2[half:half + 64, :]).then_inc(e_w, 1)

            def sums_e(i):
                S = stage_e
                for q in range(2):
                    for jj in range(HALF):
                        j = HALF * q + jj
                        radial(*two_on(i, j))
                        if jj == 0:
                            edge_scalars(*next_half(i, q))
                        if jj == 1:
                            key_transposes(S, *next_half(i, q))
                            hidden(*next_half(i, q))
                        same_j, m, o = same[:, j % 2, :], parts[:, j % 2, :], bank[2 + j % 2]
                        pe.wait_ge(S["same"], i * RING + j + 1)
                        pe.wait_ge(S["parts"], i * RING + j + 1)
                        wait(pe, S["out"], i * RING + j - 1)
                        mm(o[:, 0:DM], same_j, m[:, 0:DM], stop=False)
                        for k in range(1, 3):
                            last = mm(o[:, S0:96], same_j, m[:, S0 + MID1 * k:S0 + MID1 * k + V0], start=False,
                                      stop=k == 2)
                        last.then_inc(S["sum"], 1)

            edge_scalars(0, 0)
            key_transposes(stage_e, 0, 0)
            hidden(0, 0)
            radial(0, 0)
            radial(0, 1)
            looped(pe, STEPS, sums_e)

            def transpose_f(n, h, b):
                pe.wait_ge(f_sum, n + 1)
                wait(pe, f_Ts, n - 1)
                for c in range(4):
                    last = nc.tensor.transpose(bank[b][0:96, NP * c:NP * (c + 1)], summed[:, b, 96 * c:96 * (c + 1)],
                                               ident[0:NP, 0:NP])
                last.then_inc(f_T, 1)

            def output_maps(n, h, b, following):
                following()
                pe.wait_ge(f_Ts, n + 1)
                wait(pe, f_out, n - 1)
                o = bank[2 + b][0:NP, :]
                mm(o[:, 0:1 + S0], sumT[:, b, 0:NP], WS[:, :])
                for k in range(3):
                    last = mm(o[:, 65 + V0 * k:65 + V0 * (k + 1)], sumT[:, b, NP * (k + 1):NP * (k + 2)], WV[:, :])
                last.then_inc(f_mm, 1)

            pipelined(pe, transpose_f, output_maps)

        @block.scalar
        def _(act):
            def copy(o, a):
                return nc.scalar.activation(o, a, ACT.Copy)

            def transposed_a(n, h, b):
                act.wait_ge(a_T, n + 1)
                wait(act, a_mm, n - 1)
                copy(xT[0:S0, b, 0:NP], bank[b][0:S0, 0:NP])
                copy(xT[0:96, b, NP:2 * NP], bank[b][0:96, NP:2 * NP]).then_inc(a_Ts, 1)

            def products(n, h, b, following):
                following()
                act.wait_ge(a_mm, n + 1)
                wait(act, a_st[b], 16 * h)
                copy(nout[:, b, 0:512], bank[2 + 2 * b][0:NP, :])
                copy(nout[:, b, 512:DP], bank[3 + 2 * b][0:NP, 0:V0]).then_inc(a_out, 1)

            pipelined(act, transposed_a, products)

            def sums_out(S, i, j, width, settled, clears):
                n = len(settled)
                act.wait_ge(S["sum"], i * RING + j + 1)
                wait_adds(act, settled[j % n], clears, (i - 1) * (RING // n) + j // n + 1)
                copy(sums[:, j, 0:width], bank[2 + j % 2][:, 0:width]).then_inc(S["out"], 1)

            def sums_b(i):
                for j in range(RING):
                    sums_out(stage_b, i, j, D, settled0, C0)

            looped(act, STEPS, sums_b)

            def transposed_c(n, h, b):
                act.wait_ge(c_T, n + 1)
                wait(act, c_R, n - 1)
                copy(xT[0:S0, b, 0:NP], bank[7][0:S0, 0:NP])
                copy(xT[0:S0, b, 2 * NP:3 * NP], bank[7][0:S0, 2 * NP:3 * NP])
                copy(xT[0:96, b, NP:2 * NP], bank[7][0:96, NP:2 * NP]).then_inc(c_Ts, 1)

            def tensor_product(n, h, b, following):
                for g in range(10):
                    act.wait_ge(c_zT, 10 * n + g + 1)
                    wait(act, c_M, 10 * n + g - 3)
                    copy(zzT[:, g % 4, :], bank[4 + g % 2][:, 0:4 * NP]).then_inc(c_zTs, 1)
                    if g == 7:
                        following()
                act.wait_ge(c_var, n + 1)
                nc.scalar.activation(sd[:, :], mv[:, 1:2], ACT.Sqrt, bias=eps[0:NP, 0:1]).then_inc(c_sd, 1)
                act.wait_ge(c_xn, n + 1)
                act.dma_start(rows(normed, n), nout[:, b, 0:D]).then_inc(c_st[b], 16)

            pipelined(act, transposed_c, tensor_product)

            def transposed_d(n, h, b):
                act.wait_ge(d_T, n + 1)
                wait(act, d_mm, n - 1)
                copy(xT[0:S0, b, 0:NP], bank[b][0:S0, 0:NP])
                copy(xT[0:96, b, NP:2 * NP], bank[b][0:96, NP:2 * NP]).then_inc(d_Ts, 1)

            def layer1_maps(h):
                for b in range(2):
                    transposed_d(2 * h + b, h, b)

            looped(act, NT // 2, layer1_maps)

            def scalars_out(i, q):
                act.wait_ge(e_esT, 2 * i + q + 1)
                copy(esT[:, :], bank[4][0:HW, 0:P]).then_inc(e_esTs, 1)

            def silu(i, q):
                act.wait_ge(e_h, 2 * i + q + 1)
                wait(act, e_w, i * RING + HALF * q - HALF)
                nc.scalar.activation(hT[:, q, :, :].rearrange("p a n -> p (a n)"), bank[4][:, P:3 * P],
                                     ACT.Silu).then_inc(e_hs, 1)

            def scale_weights(i, j):
                if j % HALF == 0:
                    act.wait_ge(stage_e["key"], 2 * i + j // HALF + 1)
                act.wait_ge(e_w, i * RING + j + 1)
                wait(act, stage_e["parts"], i * RING + j - 3)
                for k in range(4):
                    w = bank[5 + j % 2][:, 0:96] if k == 0 else bank[5 + j % 2][:, 96:192]
                    last = nc.scalar.activation(scaled[:, j % 4, k, :], w, ACT.Copy,
                                                scale=shc[:, 4 * j + k:4 * j + k + 1])
                last.then_inc(e_ws, 1)

            def sums_e(i):
                for q in range(2):
                    for jj in range(HALF):
                        j = HALF * q + jj
                        scale_weights(*two_on(i, j))
                        if jj == 0:
                            scalars_out(*next_half(i, q))
                        if jj == 1:
                            silu(*next_half(i, q))
                        sums_out(stage_e, i, j, DM, settled1, C1)

            scalars_out(0, 0)
            silu(0, 0)
            scale_weights(0, 0)
            scale_weights(0, 1)
            looped(act, STEPS, sums_e)

            def transposed_f(n, h, b):
                act.wait_ge(f_T, n + 1)
                wait(act, f_mm, n - 1)
                copy(sumT[:, b, :], bank[b][0:96, 0:4 * NP]).then_inc(f_Ts, 1)

            def finish(n, h, b, following):
                following()
                act.wait_ge(f_var, n + 1)
                nc.scalar.activation(sd[:, :], mv[:, 1:2], ACT.Sqrt, bias=eps[0:NP, 0:1]).then_inc(f_sd, 1)

            pipelined(act, transposed_f, finish)


_NAMES = ["x", "src", "dst", "edge_attr_16", "edge_attr_4", "node_vec1", "L0_gnn_wm000", "L0_gnn_wm011",
          "L0_gnn_wm101", "L0_gnn_wm110", "L0_gnn_lm0", "L0_gnn_lm1", "L0_gnn_wu000", "L0_gnn_wu011", "L0_gnn_wu101",
          "L0_gnn_wu110", "L0_gnn_lu0", "L0_gnn_lu1", "L1_gnn_Wfc1", "L1_gnn_Wfc2", "L1_gnn_Wsc0", "L1_gnn_Wsc1",
          "L1_gnn_Wl1_0", "L1_gnn_Wl1_1", "L1_gnn_Wl2_s", "L1_gnn_Wl2_v", "L1_gnn_Wa"]


def kernel(**inputs):
    import numpy as _np
    import concourse.bacc as _bacc
    from concourse import mybir as _mybir
    from concourse.bass_utils import run_bass_kernel_spmd as _run

    nc = _bacc.Bacc("TRN2", target_bir_lowering=False, num_devices=1)
    arrays, args = {}, []
    for name in _NAMES:
        a = _np.ascontiguousarray(inputs[name])
        arrays[f"in_{name}_dram"] = a
        args.append(nc.dram_tensor(f"in_{name}_dram", a.shape, _mybir.dt.from_np(a.dtype), kind="ExternalInput").ap())
    out = nc.dram_tensor("out_dram", (N, D), _mybir.dt.from_np(_np.dtype("float32")), kind="ExternalOutput").ap()
    program(nc, *args, out)
    r = _run(nc, [arrays], core_ids=[0])
    return r.results[0]["out_dram"]
```

```python
import concourse.bass as bass
from concourse import mybir
from contextlib import ExitStack
import numpy as np

N, D, E = 12500, 160, 212500
S0, V0 = 64, 32
P = 128
FULL = E // P
TAIL = E - P * FULL
HALF = 4
RING = 2 * HALF
STEPS = -(-(FULL + 1) // RING)
T = STEPS * RING
NP = 125
NT = N // NP
PAIR = 2 * NP
NU = N // PAIR
ROWS = N + P
DP = D + D + 3 * S0 + V0
GP, GA, GD = range(0, 4), range(4, 5), range(5, 8)
DM = 4 * 96 + 1
MAPS = 1 + D
ACC0, ACC1 = 4, 2
CLEARS0, CLEARS1 = ACC0 * (NU + 1), ACC1 * (NT + 1)
assert NT * NP == N and NU * PAIR == N and NU % 2 == 0 and T * P >= E
I3, F96, F5120, F4096 = 1 / np.sqrt(3.0), 1 / np.sqrt(96.0), 1 / np.sqrt(5120.0), 1 / 64.0
R32 = 1 / np.sqrt(32.0)
EPS = 1e-5


def program(nc, x, src, dst, attr16, attr4, nvec, wm000, wm011, wm101, wm110, lm0, lm1,
            wu000, wu011, wu101, wu110, lu0, lu1, wfc1, wfc2, wsc0, wsc1, wl10, wl11, wl2s, wl2v, wa, out):
    f32, i32, u32 = mybir.dt.float32, mybir.dt.int32, mybir.dt.uint32
    ALU, ACT, AX = mybir.AluOpType, mybir.ActivationFunctionType, mybir.AxisListType
    ctx = ExitStack()
    with ctx:
        def sb(name, shape, dt=f32):
            return ctx.enter_context(nc.sbuf_tensor(name, shape, dt))

        def sem(name):
            return ctx.enter_context(nc.semaphore(name))

        def sems(name, n):
            return [sem(f"{name}{i}") for i in range(n)]

        def dram(name, shape):
            return nc.dram_tensor(name, shape, f32, kind="Internal").ap()

        prodtab = dram("prodtab", [N, DP])
        normed = dram("normed", [N, D])
        ftab = dram("ftab", [N, D])
        basetab = dram("basetab", [N, D])
        acc0 = [dram(f"acc0_{c}", [ROWS, D]) for c in range(ACC0)]
        acc1 = [dram(f"acc1_{c}", [ROWS, DM]) for c in range(ACC1)]

        ident = sb("ident", [P, P])
        before = sb("before", [P, P])
        trash = sb("trash", [P, 1])
        trash_i = sb("trash_i", [P, 1], i32)
        eps = sb("eps", [P, 1])
        W0 = sb("W0", [S0, 160])
        W1 = sb("W1", [96, 96 + 96 + 3 * S0])
        WU0 = sb("WU0", [P, 32, S0])
        WU011 = sb("WU011", [S0, V0 * V0])
        WU101 = sb("WU101", [S0, V0 * V0])
        WU110 = sb("WU110", [P, 8, S0])
        LU0 = sb("LU0", [S0, S0])
        LU1 = sb("LU1", [96, 96])
        WN0 = sb("WN0", [S0, 2, S0])
        WN1 = sb("WN1", [96, 2, 96])
        WF1 = sb("WF1", [HALF * 16, 2, P])
        WF2 = sb("WF2", [P, 192])
        WO0 = sb("WO0", [P, MAPS])
        WO1 = sb("WO1", [P, 2 * V0])
        WO2 = sb("WO2", [P, 2 * V0])

        src_i = sb("src_i", [P, T + RING], i32)
        dst_i = sb("dst_i", [P, T + RING], i32)
        src_f = sb("src_f", [P, T + RING])
        dst_f = sb("dst_f", [P, T + RING])
        sh = sb("sh", [P, (T + RING) * 4])

        xin = sb("xin", [NP, 4, D])
        xc = sb("xc", [NP, 4, D])
        xT = sb("xT", [96, 2, 3 * NP])
        nv = sb("nv", [NP, 4])
        nout = sb("nout", [NP, 2, 2 * DP])
        arena = sb("arena", [P, 3 * S0 * V0])
        zs = sb("zs", [NP, S0 * S0])
        zeros = sb("zeros", [P, DM])
        zz = sb("zz", [NP, 3, V0, V0])
        zzs = sb("zzs", [NP, V0, V0])
        zzT = sb("zzT", [P, 4, 4 * NP])
        agg = sb("agg", [NP, 2, ACC0 * D])
        pair = sb("pair", [NP, 2, D])
        ac = sb("ac", [NP, 2, D])
        r1 = sb("r1", [NP, 96])
        linear = sb("linear", [NP, D])
        y = sb("y", [NP, 2, D])
        st6 = sb("st6", [NP, 2, 6])
        mv = sb("mv", [NP, 2, 2])
        sd = sb("sd", [NP, 2])
        rstd = sb("rstd", [NP, 2])
        gain = sb("gain", [NP, 8])
        pT = zzT[0:96, 0:2, :]
        sumT = zzT[:, :, 0:3 * NP]
        agg1 = zs[:, 0:2 * ACC1 * 2 * DM].rearrange("p (s c d) -> p s c d", s=2, c=ACC1)
        summed = zz[:, :, :, :].rearrange("p a u v -> p (a u v)")[:, 0:4 * DM].rearrange("p (s b d) -> p s b d", s=2, b=2)

        gathered0 = arena[:, 0:RING * DP].rearrange("p (j d) -> p j d", j=RING)
        gathered1 = arena[:, 0:RING * D].rearrange("p (j d) -> p j d", j=RING)
        gidx = sb("gidx", [P, RING], i32)
        sidx = sb("sidx", [P, RING], i32)
        keyc = sb("keyc", [P, RING])
        shc = sb("shc", [P, RING * 4])
        toff = sb("toff", [P, RING])
        prev = sb("prev", [P, RING])
        moved = sb("moved", [P, RING])
        same = sb("same", [P, 2, P])
        junk = sb("junk", [P, P])
        parts = sb("parts", [P, 2, 2 * D + 3 * S0])
        sums = sb("sums", [P, RING, DM])
        es = sb("es", [P, 2, HALF * 16])
        esT = sb("esT", [HALF * 16, P])
        hT = sb("hT", [P, 2, 2, P])
        scaled = zzT[:, :, 0:4 * 96].rearrange("p j (k u) -> p j k u", k=4)

        bank = [ctx.enter_context(nc.psum_tensor(f"bank{i}", [P, 512], f32)) for i in range(8)]

        w_a = sem("w_a")
        w_in = sem("w_in")
        w_const = sem("w_const")
        w_zero = sem("w_zero")
        w_pad = sem("w_pad")
        w_ready = sem("w_ready")
        w_step = sem("w_step")
        a_in, a_xc, a_T, a_Ts, a_mm, a_out, a_st = (sems("a_in", 2), sem("a_xc"), sem("a_T"), sem("a_Ts"), sem("a_mm"),
                                                    sem("a_out"), sems("a_st", 2))
        stage_b, stage_e = [dict(gath=sems(s + "_gath", RING), used=sem(s + "_used"), key=sem(s + "_key"),
                                 kT=sem(s + "_kT"), same=sem(s + "_same"), parts=sem(s + "_parts"),
                                 sum=sem(s + "_sum"), out=sem(s + "_out"), sidx=sem(s + "_sidx"), tmp=sem(s + "_tmp"))
                            for s in "be"]
        cleared0, cleared1 = sem("cleared0"), sem("cleared1")
        settled0 = sems("settled0_", ACC0)
        settled1 = sems("settled1_", ACC1)
        e_m1 = sem("e_m1")
        e_es, e_esT, e_esTs, e_h, e_hs, e_w, e_ws = (sems("e_es", 2), sem("e_esT"), sem("e_esTs"), sem("e_h"), sem("e_hs"),
                                                     sem("e_w"), sem("e_ws"))
        c_in, c_pair, c_prep, c_T, c_Ts, c_Y, c_Yused = (sems("c_in", 2), sem("c_pair"), sem("c_prep"),
                                                               sem("c_T"), sem("c_Ts"), sem("c_Y"), sem("c_Yused"))
        c_zT, c_zTs, c_R, c_red, c_v, c_var, c_sd, c_xn, c_st = (sem("c_zT"), sem("c_zTs"), sem("c_R"), sem("c_red"),
                                                                 sem("c_v"), sem("c_var"), sem("c_sd"), sem("c_xn"),
                                                                 sems("c_st", 2))
        c_gp, c_ga, c_gd, c_M, c_zz, c_Rs = sem("c_gp"), sem("c_ga"), sem("c_gd"), sem("c_M"), sem("c_zz"), sem("c_Rs")
        d_in, d_T, d_Ts, d_mm, d_out, d_st = (sems("d_in", 2), sem("d_T"), sem("d_Ts"), sem("d_mm"), sem("d_out"),
                                              sems("d_st", 2))
        f_base = sems("f_base", 2)
        f_in, f_sum, f_T, f_Ts, f_mm, f_v, f_var, f_sd, f_out, f_st = (
            sems("f_in", 2), sem("f_sum"), sem("f_T"), sem("f_Ts"), sem("f_mm"), sem("f_v"), sem("f_var"), sem("f_sd"),
            sem("f_out"), sems("f_st", 2))
        block = ctx.enter_context(nc.Block())

        def wait(eng, s, v):
            if not isinstance(v, int) or v > 0:
                eng.wait_ge(s, v)

        def wait_adds(eng, s, adds):
            wait(eng, s, 16 * adds)

        def plain(eng):
            eng.sem_inc(w_step, 1)

        def looped(eng, count, body):
            body(0)
            with eng.Fori(1, count) as i:
                body(i)

        def pipelined(eng, count, first, body):
            def pair_of(h):
                body(2 * h, h, 0, lambda: first(2 * h + 1, h, 1))
                if isinstance(h, int) and h == count // 2 - 1:
                    body(2 * h + 1, h, 1, lambda: None)
                else:
                    body(2 * h + 1, h, 1, lambda: first(2 * h + 2, h + 1, 0))

            first(0, 0, 0)
            pair_of(0)
            with eng.Fori(1, count // 2 - 1) as h:
                pair_of(h)
            pair_of(count // 2 - 1)

        def rows(tensor, n):
            return tensor[bass.ds(n * NP, NP), :]

        def pair_rows(tensor, n):
            return tensor[bass.ds(n * PAIR, PAIR), :].rearrange("(p r) d -> p (r d)", r=2)

        def blocks3(t, c0, w):
            return [t[32 * k:32 * k + 32, c0 + w * k:c0 + w * k + w] for k in range(3)]

        WN1f = WN1[:, :, :].rearrange("p a n -> p (a n)")
        loads_a = [
            (W0[:, 0:64], lm0), (W0[:, 64:128], wm000.rearrange("u a w -> u (a w)")),
            (W0[:, 128:160], wm011.rearrange("u a w -> u (a w)")),
        ]
        loads_a += [(b, lm1) for b in blocks3(W1, 0, 32)]
        loads_a += [(b, wm101.rearrange("u a w -> u (a w)")) for b in blocks3(W1, 96, 32)]
        loads_a += [(b, wm110.rearrange("u a w -> u (a w)")) for b in blocks3(W1, 192, 64)]
        loads = [
            (WU0[:, :, :], wu000.rearrange("u v w -> (u v) w").rearrange("(c p) w -> p c w", p=P)),
            (WU011[:, :], wu011.rearrange("u v w -> u (v w)")),
            (WU101[:, :].rearrange("v (u w) -> v u w", u=V0), wu101.rearrange("u v w -> v u w")),
            (WU110[:, :, :], wu110.rearrange("u v w -> (u v) w").rearrange("(c p) w -> p c w", p=P)),
            (LU0[:, :], lu0), (WN0[:, 0, :], wl10), (WN0[:, 1, :], wsc0),
            (WO0[0:96, 1:65], wl2s), (WO0[96:128, 65:97], wl2v[0:32, :]),
            (WO1[0:64, 0:32], wl2v[32:96, :]), (WO1[64:128, 32:64], wl2v[0:64, :]),
            (WO2[0:32, 0:32], wl2v[64:96, :]), (WO2[32:128, 32:64], wl2v),
            (src_i[:, 0:FULL], src[0:P * FULL].rearrange("(p t) -> p t", p=P)),
            (dst_i[:, 0:FULL], dst[0:P * FULL].rearrange("(p t) -> p t", p=P)),
            (src_i[0:TAIL, FULL:FULL + 1], src[P * FULL:E].rearrange("(p t) -> p t", t=1)),
            (dst_i[0:TAIL, FULL:FULL + 1], dst[P * FULL:E].rearrange("(p t) -> p t", t=1)),
            (sh[:, 0:FULL * 4], attr4[0:P * FULL, :].rearrange("(p t) a -> p (t a)", p=P)),
            (sh[0:TAIL, FULL * 4:FULL * 4 + 4], attr4[P * FULL:E, :]),
            (WO0[0:96, 0:1], wa),
        ]
        loads += [(b, lu1) for b in blocks3(LU1, 0, 32)]
        loads += [(b, wl11) for b in blocks3(WN1f, 0, 32)]
        loads += [(b, wsc1) for b in blocks3(WN1f, 96, 32)]
        loads += [(WF1[16 * j:16 * j + 16, j // 2, 64 * (j % 2):64 * (j % 2) + 64], wfc1) for j in range(HALF)]
        loads += [(WF2[r:r + 64, a:b], wfc2[:, c:c + b - a]) for r in (0, 64)
                  for a, b, c in ((0, 64, 0), (64, 96, 128), (96, 160, 64), (160, 192, 160))]
        WIN = 16 * len(loads)

        attr16_v = attr16[0:P * FULL, :].rearrange("(p t) a -> p (t a)", p=P)
        HW = HALF * 16

        def node_loads(sp, count, used, load, also=lambda n: None):
            load(0, 0)
            load(1, 1)
            with sp.Fori(0, count // 2 - 1) as h:
                for b in range(2):
                    sp.wait_ge(used, 2 * h + b + 1)
                    load(2 * h + b + 2, b)
                    also(2 * h + b)
            also(count - 2)
            also(count - 1)

        def node_stores(eng, count, ready, store):
            with eng.Fori(0, count // 2) as h:
                for b in range(2):
                    eng.wait_ge(ready, 2 * h + b + 1)
                    plain(eng)
                    store(2 * h + b, b)

        def load_pair(eng, table, n, s, landed):
            eng.dma_start(xin[:, 2 * s:2 * s + 2, :].rearrange("p b d -> p (b d)"), pair_rows(table, n)).then_inc(landed, 16)
            eng.dma_start(nv[:, 2 * s:2 * s + 2], pair_rows(nvec, n)).then_inc(landed, 16)

        def clear_spare(eng, acc, cleared):
            for c, a in enumerate(acc):
                eng.dma_start(a[N:ROWS, :], zeros[:, 0:a.shape[1]]).then_inc(cleared, 16)

        @block.sync
        def _(sp):
            sp.wait_ge(w_zero, 1)
            for to, frm in loads_a:
                sp.dma_start(to, frm).then_inc(w_a, 16)

            def clear0(n):
                for c, a in enumerate(acc0):
                    sp.dma_start(pair_rows(a, n), zeros[0:NP, 0:2 * D]).then_inc(cleared0, 16)

            node_loads(sp, NU, a_xc,
                       lambda n, s: sp.dma_start(xin[:, 2 * s:2 * s + 2, :].rearrange("p b d -> p (b d)"),
                                                 pair_rows(x, n)).then_inc(a_in[s], 16), clear0)
            clear_spare(sp, acc0, cleared0)

            for c in range(ACC0):
                sp.wait_ge(settled0[c], 16 * (T // ACC0))

            def load_c(n, b):
                sp.dma_start(xin[:, b, :], rows(x, n)).then_inc(c_in[b], 16)
                for c in range(ACC0):
                    sp.dma_start(agg[:, b, c * D:(c + 1) * D], rows(acc0[c], n)).then_inc(c_in[b], 16)

            def clear1(n):
                for c, a in enumerate(acc1):
                    sp.dma_start(rows(a, n), zeros[0:NP, :]).then_inc(cleared1, 16)

            node_loads(sp, NT, c_prep, load_c, clear1)
            clear_spare(sp, acc1, cleared1)

            for b in range(2):
                sp.wait_ge(c_st[b], 16 * (NT // 2))

            node_loads(sp, NU, d_out, lambda n, s: load_pair(sp, normed, n, s, d_in[s]))

            def load_e(i):
                for q in range(2):
                    wait(sp, e_esT, 2 * i + q - 1)
                    sp.dma_start(es[:, q, :], attr16_v[:, bass.ds((2 * i + q) * HW, HW)]).then_inc(e_es[q], 16)

            looped(sp, STEPS - 1, load_e)
            sp.wait_ge(e_esT, 2 * STEPS - 3)
            sp.dma_start(es[:, 0, :], attr16_v[:, (2 * STEPS - 2) * HW:(2 * STEPS - 1) * HW]).then_inc(e_es[0], 16)
            sp.wait_ge(e_esT, 2 * STEPS - 2)
            sp.dma_start(es[0:TAIL, 1, 0:16], attr16[P * FULL:E, :]).then_inc(e_es[1], 16)
            sp.wait_ge(e_esT, 2 * STEPS - 1)
            sp.dma_start(es[:, 0, :], attr16_v[:, 0:HW]).then_inc(e_es[0], 16)

            for c in range(ACC1):
                sp.wait_ge(settled1[c], 16 * (T // ACC1))

            def load_sums(n, s):
                for c in range(ACC1):
                    sp.dma_start(agg1[:, s, c, :], pair_rows(acc1[c], n)).then_inc(f_in[s], 16)

            node_loads(sp, NU, f_sum, load_sums)
            for s in range(2):
                sp.wait_ge(f_st[s], 16 * (NU // 2))

        def scalar_products(eng, nc_eng, n, b, g):
            wait(eng, c_zT, 10 * (n - 1) + g + 1)
            return nc_eng.tensor_tensor(zs[0:NP, 512 * g:512 * (g + 1)].rearrange("p (u v) -> p u v", v=S0),
                                        xc[:, b, 8 * g:8 * g + 8].unsqueeze(2).to_broadcast([NP, 8, S0]),
                                        ac[:, b, 0:S0].unsqueeze(1).to_broadcast([NP, 8, S0]), ALU.mult)

        def edge_traffic(pool, S, table, gathered, acc, settled, cleared, clears):
            n = len(acc)
            width = acc[0].shape[1]

            def gather(j):
                plain(pool)
                pool.indirect_dma_start(gathered[:, j, :], None, table,
                                        bass.IndirectOffsetOnAxis(ap=gidx[:, j:j + 1].bitcast(u32), axis=0)
                                        ).then_inc(S["gath"][j], 16)

            def add(i, j):
                pool.wait_ge(S["out"], i * RING + j + 1)
                if j % HALF == 0:
                    pool.wait_ge(S["sidx"], 2 * i + j // HALF + 1)
                wait_adds(pool, settled[j % n], i * (RING // n) + j // n)
                plain(pool)
                pool.indirect_dma_start(acc[j % n], bass.IndirectOffsetOnAxis(ap=sidx[:, j:j + 1].bitcast(u32), axis=0),
                                        sums[:, j, 0:width], None, compute_op=ALU.add).then_inc(settled[j % n], 16)

            def add_and_gather(i):
                for j in range(RING):
                    add(i, j)
                    pool.wait_ge(S["used"], i * RING + j + 1)
                    gather(j)

            for j in range(RING):
                gather(j)
            pool.wait_ge(cleared, 16 * clears)
            looped(pool, STEPS - 1, add_and_gather)
            for j in range(RING):
                add(STEPS - 1, j)

        @block.gpsimd
        def _(pool):
            nc.gpsimd.memset(ident[:, :], 0.0).then_inc(w_const, 1)
            nc.gpsimd.memset(before[:, :], 1.0).then_inc(w_const, 1)
            pool.wait_ge(w_const, 2)
            nc.gpsimd.affine_select(out=ident[:, :], in_=ident[:, :], compare_op=ALU.not_equal, fill=1.0, base=0,
                                    pattern=[[-1, P]], channel_multiplier=1).then_inc(w_const, 1)
            nc.gpsimd.affine_select(out=before[:, :], in_=before[:, :], compare_op=ALU.is_gt, fill=0.0, base=0,
                                    pattern=[[-1, P]], channel_multiplier=1).then_inc(w_const, 1)
            nc.gpsimd.iota(trash_i[:, :], [[0, 1]], base=N, channel_multiplier=1).then_inc(w_const, 1)

            node_stores(pool, NU, a_out,
                        lambda n, s: pool.dma_start(pair_rows(prodtab, n), nout[:, s, :]).then_inc(a_st[s], 16))

            pool.wait_ge(w_ready, 2)
            for s in range(2):
                pool.wait_ge(a_st[s], 16 * (NU // 2))
            edge_traffic(pool, stage_b, prodtab, gathered0, acc0, settled0, cleared0, CLEARS0)

            def prepare(h):
                for b in range(2):
                    n = 2 * h + b
                    pool.wait_ge(c_in[b], 16 * (1 + ACC0) * (h + 1))
                    wait(pool, c_xn, n - 1)
                    plain(pool)
                    nc.gpsimd.tensor_copy(xc[:, b, 0:S0], xin[:, b, 0:S0])
                    nc.gpsimd.tensor_copy(xc[:, b, S0:D].rearrange("p (k u) -> p k u", k=3),
                                          xin[:, b, S0:D].rearrange("p (u k) -> p k u", k=3))
                    nc.gpsimd.tensor_tensor(pair[:, 0, :], agg[:, b, 0:D], agg[:, b, D:2 * D], ALU.add)
                    nc.gpsimd.tensor_tensor(pair[:, 1, :], agg[:, b, 2 * D:3 * D], agg[:, b, 3 * D:4 * D],
                                            ALU.add).then_inc(c_pair, 1)
                    pool.wait_ge(c_pair, n + 1)
                    nc.gpsimd.tensor_tensor(ac[:, b, :], pair[:, 0, :], pair[:, 1, :], ALU.add).then_inc(c_prep, 1)
                    pool.wait_ge(c_prep, n + 1)
                    for g in GP:
                        scalar_products(pool, nc.gpsimd, n, b, g).then_inc(c_gp, 1)
                    for k in range(3):
                        xk = xc[:, b, S0 + V0 * k:S0 + V0 * (k + 1)]
                        ak = ac[:, b, S0 + V0 * k:S0 + V0 * (k + 1)]
                        last = nc.gpsimd.tensor_tensor(zz[:, k, :, :], xk.unsqueeze(2).to_broadcast([NP, V0, V0]),
                                                       ak.unsqueeze(1).to_broadcast([NP, V0, V0]), ALU.mult)
                    last.then_inc(c_zz, 1)
                    pool.wait_ge(c_zz, 2 * n + 1)
                    nc.gpsimd.tensor_tensor(zz[:, 0, :, :], zz[:, 0, :, :], zz[:, 1, :, :], ALU.add).then_inc(c_zz, 1)
                    pool.wait_ge(c_zz, 2 * n + 2)
                    wait(pool, c_zT, 10 * n)
                    nc.gpsimd.tensor_tensor(zzs[:, :, :], zz[:, 0, :, :], zz[:, 2, :, :], ALU.add).then_inc(c_gp, 1)

            looped(pool, NT // 2, prepare)

            def store_d(n, s):
                pool.dma_start(pair_rows(ftab, n), nout[:, s, 0:2 * D]).then_inc(d_st[s], 16)
                pool.dma_start(pair_rows(basetab, n), nout[:, s, 2 * D:4 * D]).then_inc(d_st[s], 16)

            node_stores(pool, NU, d_out, store_d)

            pool.wait_ge(w_ready, 3)
            for s in range(2):
                pool.wait_ge(d_st[s], 32 * (NU // 2))
            edge_traffic(pool, stage_e, ftab, gathered1, acc1, settled1, cleared1, CLEARS1)

            def sum_accumulators(h):
                for s in range(2):
                    n = 2 * h + s
                    pool.wait_ge(f_in[s], 16 * ACC1 * (h + 1))
                    wait(pool, f_v, 10 * (n - 2) + 1)
                    wait(pool, f_T, n - 1)
                    plain(pool)
                    nc.gpsimd.tensor_tensor(summed[:, s, :, :].rearrange("p b d -> p (b d)"), agg1[:, s, 0, :],
                                            agg1[:, s, 1, :], ALU.add).then_inc(f_sum, 1)

            looped(pool, NU // 2, sum_accumulators)

        def next_half(i, q):
            return (i, 1) if q == 0 else (i + 1, 0)

        def two_on(i, j):
            return (i, j + 2) if j + 2 < RING else (i + 1, j + 2 - RING)

        def stage_keys(dve, S, i, q, key_table):
            c = slice(HALF * q, HALF * (q + 1))
            wait(dve, S["sidx"], 2 * i + q - 1)
            nc.vector.tensor_copy(shc[:, 16 * q:16 * (q + 1)], sh[:, bass.ds(i * (4 * RING) + 16 * q, 16)])
            nc.vector.tensor_copy(keyc[:, c], key_table[:, bass.ds(i * RING + HALF * q, HALF)]).then_inc(S["key"], 1)
            dve.wait_ge(S["key"], 2 * i + q + 1)
            nc.vector.tensor_scalar(toff[:, c], keyc[:, c], -1.0, trash[:, 0:1], ALU.mult, ALU.add)

        def match_tile(dve, S, i, q, jj):
            j = HALF * q + jj
            if jj == 0:
                dve.wait_ge(S["kT"], 2 * i + q + 1)
            kT = bank[q][:, P * jj:P * (jj + 1)]
            wait(dve, S["same"], i * RING + j)
            nc.vector.scalar_tensor_tensor(out=junk[:, :], in0=kT, scalar=keyc[:, j:j + 1], in1=before[:, :],
                                           op0=ALU.is_equal, op1=ALU.mult, accum_out=prev[:, j:j + 1])
            wait(dve, S["sum"], i * RING + j - 1)
            nc.vector.tensor_scalar(same[:, j % 2, :], kT, keyc[:, j:j + 1], None, ALU.is_equal).then_inc(S["same"], 1)

        def next_rows(i, j, S, index_table):
            nc.vector.tensor_copy(gidx[:, j:j + 1], index_table[:, bass.ds((i + 1) * RING + j, 1)]).then_inc(S["used"], 1)

        def target_rows(dve, S, i, q, settled):
            n = len(settled)
            c = slice(HALF * q, HALF * (q + 1))
            dve.wait_ge(S["same"], i * RING + HALF * (q + 1))
            nc.vector.scalar_tensor_tensor(out=moved[:, c], in0=prev[:, c], scalar=0.0, in1=toff[:, c], op0=ALU.is_gt,
                                           op1=ALU.mult).then_inc(S["tmp"], 1)
            dve.wait_ge(S["tmp"], 2 * i + q + 1)
            for a in range(n):
                wait_adds(dve, settled[a], (i - 1) * (RING // n) + (q + 1) * (HALF // n))
            nc.vector.tensor_tensor(sidx[:, c], moved[:, c], keyc[:, c], ALU.add).then_inc(S["sidx"], 1)

        @block.vector
        def _(dve):
            for t in (zeros[:, :], W1[:, :], LU1[:, :], WN1[:, :, :], WF1[:, :, :], WO0[:, :], WO1[:, :], WO2[:, :],
                      sh[:, FULL * 4:]):
                nc.vector.memset(t, 0.0)
            nc.vector.memset(src_i[:, FULL:], 0)
            nc.vector.memset(dst_i[:, FULL:], 0)
            nc.vector.memset(eps[:, :], EPS).then_inc(w_zero, 1)
            dve.wait_ge(w_const, 5)
            dve.wait_ge(w_a, 16 * len(loads_a))
            for ap, f in ((W0[:, 0:64], 1 / 8), (W0[:, 64:160], F96), (W1[:, 0:96], R32), (W1[:, 96:192], F96),
                          (W1[:, 192:384], F96 * I3)):
                last = nc.vector.tensor_scalar(ap, ap, float(f), None, ALU.mult)
            last.then_inc(w_ready, 1)

            def rearrange_x(h):
                for s in range(2):
                    n = 2 * h + s
                    tiles = slice(2 * s, 2 * s + 2)
                    dve.wait_ge(a_in[s], 16 * (h + 1))
                    wait(dve, a_T, n - 1)
                    nc.vector.tensor_copy(xc[:, tiles, 0:S0], xin[:, tiles, 0:S0])
                    nc.vector.tensor_copy(xc[:, tiles, S0:D].rearrange("p b (k u) -> p b k u", k=3),
                                          xin[:, tiles, S0:D].rearrange("p b (u k) -> p b k u", k=3)).then_inc(a_xc, 1)

            looped(dve, NU // 2, rearrange_x)

            nc.vector.tensor_copy(trash[:, :], trash_i[:, :]).then_inc(w_pad, 1)
            dve.wait_ge(w_pad, 1)
            dve.wait_ge(w_in, WIN)
            for tab_f, tab_i in ((src_f, src_i), (dst_f, dst_i)):
                nc.vector.tensor_copy(tab_f[:, 0:FULL], tab_i[:, 0:FULL])
                nc.vector.tensor_copy(tab_f[:, FULL:], trash[:, 0:1].to_broadcast([P, T + RING - FULL])).then_inc(w_pad, 1)
            dve.wait_ge(w_pad, 3)
            nc.vector.tensor_copy(src_f[0:TAIL, FULL:FULL + 1], src_i[0:TAIL, FULL:FULL + 1])
            nc.vector.tensor_copy(dst_f[0:TAIL, FULL:FULL + 1], dst_i[0:TAIL, FULL:FULL + 1])
            for ap, f in ((WU110[:, :, :], I3 * F5120), (WU0[:, :, :], F5120), (LU0[:, :], 1 / 8), (LU1[:, :], R32),
                          (WN0[:, :, :], 1 / 8), (WN1[:, :, :], R32), (WF1[:, :, :], 1 / 4), (WF2[:, 0:160], 1 / 8),
                          (WF2[:, 160:192], I3 / 8), (WO0[:, :], F96), (WO1[:, :], F96), (WO2[:, :], F96)):
                nc.vector.tensor_scalar(ap, ap, float(f), None, ALU.mult)
            nc.vector.tensor_copy(gidx[:, :], dst_i[:, 0:RING]).then_inc(w_ready, 1)

            def edges_b(i):
                S = stage_b
                for q in range(2):
                    for jj in range(HALF):
                        j = HALF * q + jj
                        p2, g = parts[:, j % 2, :], gathered0[:, j, :]
                        e0, e1 = shc[:, 4 * j + 3:4 * j + 4], shc[:, 4 * j:4 * j + 3]
                        match_tile(dve, S, i, q, jj)
                        dve.wait_ge(S["gath"][j], 16 * (i + 1))
                        nc.vector.scalar_tensor_tensor(out=p2[:, 0:D], in0=g[:, D:2 * D], scalar=e0, in1=g[:, 0:D],
                                                       op0=ALU.mult, op1=ALU.add)
                        nc.vector.tensor_tensor(p2[:, D:D + 192].rearrange("p (k u) -> p k u", k=3),
                                                g[:, 2 * D:2 * D + 192].rearrange("p (k u) -> p k u", k=3),
                                                e1.unsqueeze(2).to_broadcast([P, 3, S0]), ALU.mult)
                        nc.vector.tensor_tensor(p2[:, D + 192:D + 288].rearrange("p (k u) -> p k u", k=3),
                                                g[:, DP - V0:DP].unsqueeze(1).to_broadcast([P, 3, V0]),
                                                e1.unsqueeze(2).to_broadcast([P, 3, V0]), ALU.mult
                                                ).then_inc(S["parts"], 1)
                        next_rows(i, j, S, dst_i)
                        if jj == 0:
                            stage_keys(dve, S, *next_half(i, q), src_f)
                    target_rows(dve, S, i, q, settled0)

            stage_keys(dve, stage_b, 0, 0, src_f)
            looped(dve, STEPS, edges_b)
            dve.wait_ge(stage_b["kT"], 2 * STEPS + 1)
            nc.vector.tensor_copy(gidx[:, :], src_i[:, 0:RING]).then_inc(w_ready, 1)

            def products_dve(n, h, b):
                dve.wait_ge(c_prep, n + 1)
                for g in GD:
                    scalar_products(dve, nc.vector, n, b, g).then_inc(c_gd, 1)

            def tensor_product(n, h, b, following):
                zv = arena[0:NP, :].rearrange("p (k r w) -> p k r w", k=3, w=V0)
                wait(dve, c_red, n)
                for c in range(4):
                    other = (ac, ac, xc, xc)[c][:, b, S0:D].rearrange("p (k u) -> p k u", k=3)
                    part = 16 * (c % 2)
                    dve.wait_ge(c_Y, 4 * n + c + 1)
                    nc.vector.tensor_tensor(
                        zv[:, :, 16 * c:16 * (c + 1), :],
                        bank[c][0:NP, :].rearrange("p (v w) -> p v w", w=V0).unsqueeze(1).to_broadcast([NP, 3, 16, V0]),
                        other[:, :, part:part + 16].unsqueeze(3).to_broadcast([NP, 3, 16, V0]),
                        ALU.mult).then_inc(c_Yused, 1)
                dve.wait_ge(c_Yused, 4 * n + 4)
                nc.vector.tensor_reduce(r1[:, :].rearrange("p (k w) -> p k w", k=3),
                                        zv.rearrange("p k r w -> p k w r"), AX.X, ALU.add).then_inc(c_red, 1)
                dve.wait_ge(c_Rs, n + 1)
                wait(dve, c_xn, n)
                nc.vector.scalar_tensor_tensor(out=y[:, 0, :], in0=xc[:, b, :], scalar=2.0, in1=linear[:, :],
                                               op0=ALU.mult, op1=ALU.add).then_inc(c_v, 1)
                dve.wait_ge(c_red, n + 1)
                dve.wait_ge(c_v, 4 * n + 1)
                nc.vector.scalar_tensor_tensor(out=y[:, 0, S0:D], in0=r1[:, :], scalar=float(F4096), in1=y[:, 0, S0:D],
                                               op0=ALU.mult, op1=ALU.add).then_inc(c_v, 1)
                dve.wait_ge(c_v, 4 * n + 2)
                nc.vector.bn_stats(st6[:, 0, :], y[:, 0, :]).then_inc(c_v, 1)
                dve.wait_ge(c_v, 4 * n + 3)
                plain(dve)
                nc.vector.bn_aggr(mv[:, 0, :], st6[:, 0, :]).then_inc(c_var, 1)
                following()
                dve.wait_ge(c_sd, n + 1)
                nc.vector.reciprocal(rstd[:, 0:1], sd[:, 0:1]).then_inc(c_v, 1)
                dve.wait_ge(c_v, 4 * n + 4)
                wait(dve, c_st[b], 16 * h)
                nc.vector.tensor_scalar(nout[:, b, 0:D], y[:, 0, :], mv[:, 0, 0:1], rstd[:, 0:1], ALU.subtract,
                                        ALU.mult).then_inc(c_xn, 1)

            pipelined(dve, NT, products_dve, tensor_product)

            def layer1_maps(h):
                for s in range(2):
                    n = 2 * h + s
                    dve.wait_ge(d_in[s], 32 * (h + 1))
                    wait(dve, d_st[s], 32 * h)
                    for b in range(2):
                        dve.wait_ge(d_mm, 2 * n + b + 1)
                        m, f, base = bank[2 + 2 * s + b], nout[:, s, D * b:D * (b + 1)], nout[:, s, D * (2 + b):D * (3 + b)]
                        g = nv[:, 2 * s + b:2 * s + b + 1]
                        for c0, w, o in ((0, S0, 0), (2 * S0, 96, S0)):
                            nc.vector.tensor_scalar(f[:, o:o + w], m[0:NP, c0:c0 + w], g, None, ALU.mult)
                            last = nc.vector.scalar_tensor_tensor(out=base[:, o:o + w], in0=m[0:NP, c0 + w:c0 + 2 * w],
                                                                  scalar=g, in1=xin[:, 2 * s + b, o:o + w],
                                                                  op0=ALU.mult, op1=ALU.add)
                    last.then_inc(d_out, 1)

            looped(dve, NU // 2, layer1_maps)

            nc.vector.memset(parts[:, :, DM - 1:DM], 1.0)

            def edges_e(i):
                S = stage_e
                for q in range(2):
                    for jj in range(HALF):
                        j = HALF * q + jj
                        m, g, w = parts[:, j % 2, :], gathered1[:, j, :], scaled[:, j % 4, :, :]
                        vec = m[:, 96:384].rearrange("p (k u) -> p k u", k=3)
                        gv = g[:, S0:D].rearrange("p (k u) -> p k u", k=3)
                        match_tile(dve, S, i, q, jj)
                        dve.wait_ge(S["gath"][j], 16 * (i + 1))
                        dve.wait_ge(e_ws, i * RING + j + 1)
                        by_k = m[:, DM:DM + 96].rearrange("p (k u) -> p k u", k=3)
                        nc.vector.tensor_tensor(by_k, w[:, 1:4, S0:96], gv, ALU.mult).then_inc(e_m1, 1)
                        nc.vector.tensor_tensor(m[:, 0:4 * 96].rearrange("p (k u) -> p k u", k=4)[:, :, 0:S0],
                                                w[:, :, 0:S0], g[:, 0:S0].unsqueeze(1).to_broadcast([P, 4, S0]),
                                                ALU.mult)
                        nc.vector.tensor_tensor(vec[:, :, S0:96], w[:, 0:1, S0:96].to_broadcast([P, 3, V0]), gv,
                                                ALU.mult)
                        dve.wait_ge(e_m1, i * RING + j + 1)
                        nc.vector.tensor_reduce(m[:, S0:96], m[:, DM:DM + 96].rearrange("p (k u) -> p u k", k=3), AX.X,
                                                ALU.add).then_inc(S["parts"], 1)
                        next_rows(i, j, S, src_i)
                        if jj == 0:
                            stage_keys(dve, S, *next_half(i, q), dst_f)
                    target_rows(dve, S, i, q, settled1)

            stage_keys(dve, stage_e, 0, 0, dst_f)
            looped(dve, STEPS, edges_e)

            def finish(h):
                for s in range(2):
                    n = 2 * h + s
                    dve.wait_ge(f_sum, n + 1)
                    wait(dve, f_out, n)
                    dve.wait_ge(f_base[s], 32 * (h + 1))
                    nc.vector.tensor_scalar(gain[:, 0:2], summed[:, s, :, DM - 1], 1.0, None, ALU.max).then_inc(f_v, 1)
                    dve.wait_ge(f_v, 10 * n + 1)
                    nc.vector.reciprocal(gain[:, 2:4], gain[:, 0:2]).then_inc(f_v, 1)
                    dve.wait_ge(f_v, 10 * n + 2)
                    nc.vector.tensor_tensor(gain[:, 4:6], gain[:, 2:4], nv[:, 2 * s:2 * s + 2], ALU.mult).then_inc(f_v, 1)
                    dve.wait_ge(f_v, 10 * n + 3)
                    dve.wait_ge(f_mm, n + 1)
                    m = [bank[4 + s][0:NP, MAPS * b:MAPS * (b + 1)] for b in range(2)]
                    for b in range(2):
                        nc.vector.tensor_scalar(gain[:, 6 + b:7 + b], m[b][:, 0:1], gain[:, 4 + b:5 + b],
                                                gain[:, 4 + b:5 + b], ALU.mult, ALU.mult).then_inc(f_v, 1)
                    for b in range(2):
                        dve.wait_ge(f_v, 10 * n + 4 + b)
                        nc.vector.scalar_tensor_tensor(out=y[:, b, :], in0=m[b][:, 1:MAPS], scalar=gain[:, 6 + b:7 + b],
                                                       in1=xin[:, 2 * s + b, :], op0=ALU.mult, op1=ALU.add
                                                       ).then_inc(f_v, 1)
                    for b in range(2):
                        dve.wait_ge(f_v, 10 * n + 6 + b)
                        nc.vector.bn_stats(st6[:, b, :], y[:, b, :]).then_inc(f_v, 1)
                    for b in range(2):
                        dve.wait_ge(f_v, 10 * n + 8 + b)
                        plain(dve)
                        nc.vector.bn_aggr(mv[:, b, :], st6[:, b, :]).then_inc(f_var, 1)
                    dve.wait_ge(f_sd, n + 1)
                    nc.vector.reciprocal(rstd[:, :], sd[:, :]).then_inc(f_v, 1)
                    dve.wait_ge(f_v, 10 * n + 10)
                    wait(dve, f_st[s], 16 * h)
                    for b in range(2):
                        o = nout[:, s, D * b:D * (b + 1)]
                        nc.vector.tensor_scalar(o[:, 0:S0], y[:, b, 0:S0], mv[:, b, 0:1], rstd[:, b:b + 1],
                                                ALU.subtract, ALU.mult)
                        last = nc.vector.tensor_scalar(o[:, S0:D].rearrange("p (u k) -> p k u", k=3),
                                                       y[:, b, S0:D].rearrange("p (k u) -> p k u", k=3), mv[:, b, 0:1],
                                                       rstd[:, b:b + 1], ALU.subtract, ALU.mult)
                    last.then_inc(f_out, 1)

            looped(dve, NU // 2, finish)

        def to_node_major(pe, src_tile, psum):
            plain(nc.tensor)
            nc.tensor.transpose(psum[0:S0, 0:NP], src_tile[:, 0:S0], ident[0:NP, 0:NP])
            return nc.tensor.transpose(psum[0:96, NP:2 * NP], src_tile[:, S0:D], ident[0:NP, 0:NP])

        def transpose_pair(src_tiles, psum):
            for b in range(2):
                plain(nc.tensor)
                nc.tensor.transpose(psum[0:S0, NP * b:NP * (b + 1)], src_tiles[:, b, 0:S0], ident[0:NP, 0:NP])
                last = nc.tensor.transpose(psum[0:96, NP * (2 + b):NP * (3 + b)], src_tiles[:, b, S0:D], ident[0:NP, 0:NP])
            return last

        def mm(o, a, c, start=True, stop=True):
            return nc.tensor.matmul(o, a, c, start=start, stop=stop)

        @block.tensor
        def _(pe):
            pe.wait_ge(w_ready, 1)

            def transpose_a(n, h, s):
                pe.wait_ge(a_xc, n + 1)
                wait(pe, a_Ts, n - 1)
                transpose_pair(xc[:, 2 * s:2 * s + 2, :], bank[s]).then_inc(a_T, 1)

            def products(n, h, s, following):
                following()
                pe.wait_ge(a_Ts, n + 1)
                wait(pe, a_out, n - 1)
                for b in range(2):
                    mm(bank[6 + s][0:NP, 160 * b:160 * (b + 1)], pT[0:S0, s, NP * b:NP * (b + 1)], W0[:, :])
                    mm(bank[2 + 2 * s + b][0:NP, 0:384], pT[:, s, NP * (2 + b):NP * (3 + b)], W1[:, :]).then_inc(a_mm, 1)

            pipelined(pe, NU, transpose_a, products)
            pe.wait_ge(w_ready, 2)

            def key_transposes(S, i, q):
                pe.wait_ge(S["key"], 2 * i + q + 1)
                for jj in range(HALF):
                    j = HALF * q + jj
                    last = nc.tensor.transpose(bank[q][:, P * jj:P * (jj + 1)], keyc[:, j:j + 1].to_broadcast([P, P]),
                                               ident[:, :])
                last.then_inc(S["kT"], 1)

            def sums_b(i):
                S = stage_b
                for q in range(2):
                    for jj in range(HALF):
                        j = HALF * q + jj
                        same_j, p2, o = same[:, j % 2, :], parts[:, j % 2, :], bank[2 + j % 2]
                        pe.wait_ge(S["same"], i * RING + j + 1)
                        pe.wait_ge(S["parts"], i * RING + j + 1)
                        wait(pe, S["out"], i * RING + j - 1)
                        mm(o[:, 0:D], same_j, p2[:, 0:D], stop=False)
                        for k in range(3):
                            mm(o[:, 0:S0], same_j, p2[:, D + S0 * k:D + S0 * (k + 1)], start=False, stop=False)
                        mm(o[:, S0:D], same_j, p2[:, D + 192:D + 288], start=False).then_inc(S["sum"], 1)
                        if jj == 1:
                            key_transposes(S, *next_half(i, q))

            key_transposes(stage_b, 0, 0)
            looped(pe, STEPS, sums_b)

            def transpose_c(n, h, b):
                pe.wait_ge(c_prep, n + 1)
                wait(pe, c_Ts, n)
                plain(pe)
                nc.tensor.transpose(bank[7][0:S0, 2 * NP:3 * NP], ac[:, b, 0:S0], ident[0:NP, 0:NP])
                to_node_major(pe, xc[:, b, :], bank[7]).then_inc(c_T, 1)

            def transpose_group(n, g):
                for made, owned in ((c_gp, GP), (c_ga, GA), (c_gd, GD)):
                    if g in owned:
                        pe.wait_ge(made, (len(owned) + (made is c_gp)) * n + g - owned[0] + 1)
                if g >= 8:
                    pe.wait_ge(c_gp, (len(GP) + 1) * (n + 1))
                wait(pe, c_zTs, 10 * n + g - 1)
                of = zs[0:NP, 512 * g:512 * (g + 1)] if g < 8 else \
                    zzs[:, :, :].rearrange("p u v -> p (u v)")[:, 512 * (g - 8):512 * (g - 7)]
                for c in range(4):
                    last = nc.tensor.transpose(bank[4 + g % 2][:, NP * c:NP * (c + 1)], of[:, P * c:P * (c + 1)],
                                               ident[0:NP, 0:NP])
                last.then_inc(c_zT, 1)

            def contract_group(n, g):
                pe.wait_ge(c_zTs, 10 * n + g + 1)
                if g == 0:
                    wait(pe, c_Rs, n)
                for c in range(4):
                    weights = WU0[:, 4 * g + c, :] if g < 8 else WU110[:, 4 * (g - 8) + c, :]
                    last = mm(bank[6][0:NP, 0:S0], zzT[:, g % 4, NP * c:NP * (c + 1)], weights,
                              start=g == 0 and c == 0, stop=False)
                last.then_inc(c_M, 1)

            def tensor_product(n, h, b, following):
                pe.wait_ge(c_Ts, n + 1)
                x0T, x1T, a0T = xT[0:S0, b, 0:NP], xT[0:96, b, NP:2 * NP], xT[0:S0, b, 2 * NP:3 * NP]
                for c in range(4):
                    wait(pe, c_Yused, 4 * (n - 1) + c + 1)
                    w = WU011 if c < 2 else WU101
                    mm(bank[c][0:NP, :], x0T if c < 2 else a0T, w[:, 512 * (c % 2):512 * (c % 2 + 1)]).then_inc(c_Y, 1)
                for g in range(11):
                    if g < 10:
                        transpose_group(n, g)
                    if g == 7:
                        following()
                    if g > 0:
                        contract_group(n, g - 1)
                mm(bank[6][0:NP, 0:S0], x0T, LU0[:, :], start=False)
                mm(bank[6][0:NP, S0:D], x1T, LU1[:, :]).then_inc(c_R, 1)

            pipelined(pe, NT, transpose_c, tensor_product)

            def transpose_d(n, h, s):
                pe.wait_ge(d_in[s], 32 * (h + 1))
                wait(pe, d_Ts, n - 1)
                transpose_pair(xin[:, 2 * s:2 * s + 2, :], bank[s]).then_inc(d_T, 1)

            def layer1_maps(h):
                for s in range(2):
                    n = 2 * h + s
                    transpose_d(n, h, s)
                    pe.wait_ge(d_Ts, n + 1)
                    wait(pe, d_out, n - 1)
                    for b in range(2):
                        o = bank[2 + 2 * s + b][0:NP, :]
                        mm(o[:, 0:2 * S0], pT[0:S0, s, NP * b:NP * (b + 1)], WN0[:, :, :].rearrange("p a n -> p (a n)"))
                        mm(o[:, 2 * S0:2 * D], pT[:, s, NP * (2 + b):NP * (3 + b)], WN1f).then_inc(d_mm, 1)

            looped(pe, NU // 2, layer1_maps)

            def edge_scalars(i, q):
                pe.wait_ge(e_es[q], 16 * (i + 1))
                wait(pe, e_esTs, 2 * i + q)
                plain(pe)
                nc.tensor.transpose(bank[4][0:HW, 0:P], es[:, q, :], ident[:, :]).then_inc(e_esT, 1)

            def hidden(i, q):
                pe.wait_ge(e_esTs, 2 * i + q + 1)
                wait(pe, e_hs, 2 * i + q)
                for pr in range(2):
                    last = mm(bank[4][:, P * (1 + pr):P * (2 + pr)], WF1[:, pr, :], esT[:, :])
                last.then_inc(e_h, 1)

            def radial(i, j):
                if j % HALF == 0:
                    pe.wait_ge(e_hs, 2 * i + j // HALF + 1)
                wait(pe, e_ws, i * RING + j - 1)
                half = 64 * (j % 2)
                mm(bank[5 + j % 2][:, 0:192], hT[half:half + 64, j // HALF, (j % HALF) // 2, :],
                   WF2[half:half + 64, :]).then_inc(e_w, 1)

            def sums_e(i):
                S = stage_e
                for q in range(2):
                    for jj in range(HALF):
                        j = HALF * q + jj
                        radial(*two_on(i, j))
                        if jj == 0:
                            edge_scalars(*next_half(i, q))
                        if jj == 1:
                            key_transposes(S, *next_half(i, q))
                            hidden(*next_half(i, q))
                        same_j, m, o = same[:, j % 2, :], parts[:, j % 2, :], bank[2 + j % 2]
                        pe.wait_ge(S["same"], i * RING + j + 1)
                        pe.wait_ge(S["parts"], i * RING + j + 1)
                        wait(pe, S["out"], i * RING + j - 1)
                        mm(o[:, 0:DM], same_j, m[:, 0:DM]).then_inc(S["sum"], 1)

            pe.wait_ge(d_out, NU)
            edge_scalars(0, 0)
            key_transposes(stage_e, 0, 0)
            hidden(0, 0)
            radial(0, 0)
            radial(0, 1)
            looped(pe, STEPS, sums_e)

            def transpose_f(n, h, s):
                pe.wait_ge(f_sum, n + 1)
                wait(pe, f_Ts, n - 1)
                for b in range(2):
                    for c in range(3):
                        last = nc.tensor.transpose(bank[2 * s + b][:, NP * c:NP * (c + 1)],
                                                   summed[:, s, b, P * c:P * (c + 1)], ident[0:NP, 0:NP])
                last.then_inc(f_T, 1)

            def output_maps(h):
                for s in range(2):
                    n = 2 * h + s
                    transpose_f(n, h, s)
                    pe.wait_ge(f_Ts, n + 1)
                    wait(pe, f_out, n - 1)
                    for b in range(2):
                        o, a = bank[4 + s][0:NP, MAPS * b:MAPS * (b + 1)], sumT[:, 2 * s + b, :]
                        mm(o, a[:, 0:NP], WO0[:, :], stop=False)
                        mm(o[:, 65:129], a[:, NP:2 * NP], WO1[:, :], start=False, stop=False)
                        last = mm(o[:, 97:161], a[:, 2 * NP:3 * NP], WO2[:, :], start=False)
                    last.then_inc(f_mm, 1)

            looped(pe, NU // 2, output_maps)

        @block.scalar
        def _(act):
            def copy(o, a):
                return nc.scalar.activation(o, a, ACT.Copy)

            act.wait_ge(w_zero, 1)
            for to, frm in loads:
                act.dma_start(to, frm).then_inc(w_in, 16)

            def copy_pair(s):
                copy(pT[0:S0, s, 0:2 * NP], bank[s][0:S0, 0:2 * NP])
                return copy(pT[:, s, 2 * NP:4 * NP], bank[s][0:96, 2 * NP:4 * NP])

            def transposed_a(n, h, s):
                act.wait_ge(a_T, n + 1)
                wait(act, a_mm, 2 * (n - 1))
                copy_pair(s).then_inc(a_Ts, 1)

            def products(n, h, s, following):
                following()
                o = nout[:, s, :].rearrange("p (b d) -> p b d", b=2)
                act.wait_ge(a_mm, 2 * n + 1)
                wait(act, a_st[s], 16 * h)
                for b in range(2):
                    act.wait_ge(a_mm, 2 * n + b + 1)
                    copy(o[:, b, S0:D], bank[2 + 2 * s + b][0:NP, 0:96])
                    copy(o[:, b, D + S0:DP - V0], bank[2 + 2 * s + b][0:NP, 96:384])
                m = bank[6 + s][0:NP, 0:320].rearrange("p (b c) -> p b c", b=2)
                for a in range(2):
                    copy(o[:, :, D * a:D * a + S0], m[:, :, S0 * a:S0 * (a + 1)])
                copy(o[:, :, DP - V0:DP], m[:, :, 2 * S0:2 * S0 + V0]).then_inc(a_out, 1)

            pipelined(act, NU, transposed_a, products)

            def sums_out(S, i, j, width, settled):
                n = len(settled)
                act.wait_ge(S["sum"], i * RING + j + 1)
                wait_adds(act, settled[j % n], (i - 1) * (RING // n) + j // n + 1)
                copy(sums[:, j, 0:width], bank[2 + j % 2][:, 0:width]).then_inc(S["out"], 1)

            def sums_b(i):
                for j in range(RING):
                    sums_out(stage_b, i, j, D, settled0)

            looped(act, STEPS, sums_b)

            def transposed_c(n, h, b):
                act.wait_ge(c_T, n + 1)
                wait(act, c_R, n - 1)
                copy(xT[0:S0, b, 0:NP], bank[7][0:S0, 0:NP])
                copy(xT[0:S0, b, 2 * NP:3 * NP], bank[7][0:S0, 2 * NP:3 * NP])
                copy(xT[0:96, b, NP:2 * NP], bank[7][0:96, NP:2 * NP]).then_inc(c_Ts, 1)

            def tensor_product(n, h, b, following):
                root(n - 1)
                for g in range(10):
                    act.wait_ge(c_zT, 10 * n + g + 1)
                    wait(act, c_M, 10 * n + g - 3)
                    copy(zzT[:, g % 4, :], bank[4 + g % 2][:, 0:4 * NP]).then_inc(c_zTs, 1)
                    if g == 5:
                        store_normed(n - 1, 1 - b)
                    if g == 7:
                        following()
                act.wait_ge(c_R, n + 1)
                wait(act, c_v, 4 * (n - 1) + 1)
                copy(linear[:, :], bank[6][0:NP, 0:D]).then_inc(c_Rs, 1)
                if not (isinstance(n, int) and n == NT - 1):
                    products_act(n + 1, 1 - b)

            def products_act(n, b):
                act.wait_ge(c_prep, n + 1)
                for g in GA:
                    wait(act, c_zT, 10 * (n - 1) + g + 1)
                    for u in range(8 * g, 8 * g + 8):
                        last = nc.scalar.activation(zs[0:NP, S0 * u:S0 * (u + 1)], ac[:, b, 0:S0], ACT.Copy,
                                                    scale=xc[:, b, u:u + 1])
                    last.then_inc(c_ga, 1)

            def root(n):
                if not (isinstance(n, int) and n < 0):
                    act.wait_ge(c_var, n + 1)
                    nc.scalar.activation(sd[:, 0:1], mv[:, 0, 1:2], ACT.Sqrt, bias=eps[0:NP, 0:1]).then_inc(c_sd, 1)

            def store_normed(n, b):
                if not (isinstance(n, int) and n < 0):
                    act.wait_ge(c_xn, n + 1)
                    act.dma_start(rows(normed, n), nout[:, b, 0:D]).then_inc(c_st[b], 16)

            products_act(0, 0)
            pipelined(act, NT, transposed_c, tensor_product)
            root(NT - 1)
            store_normed(NT - 1, 1)

            def transposed_d(h):
                for s in range(2):
                    n = 2 * h + s
                    act.wait_ge(d_T, n + 1)
                    wait(act, d_mm, 2 * (n - 1))
                    copy_pair(s).then_inc(d_Ts, 1)

            looped(act, NU // 2, transposed_d)

            def scalars_out(i, q):
                act.wait_ge(e_esT, 2 * i + q + 1)
                copy(esT[:, :], bank[4][0:HW, 0:P]).then_inc(e_esTs, 1)

            def silu(i, q):
                act.wait_ge(e_h, 2 * i + q + 1)
                wait(act, e_w, i * RING + HALF * q - HALF)
                nc.scalar.activation(hT[:, q, :, :].rearrange("p a n -> p (a n)"), bank[4][:, P:3 * P],
                                     ACT.Silu).then_inc(e_hs, 1)

            def scale_weights(i, j):
                if j % HALF == 0:
                    act.wait_ge(stage_e["key"], 2 * i + j // HALF + 1)
                act.wait_ge(e_w, i * RING + j + 1)
                wait(act, stage_e["parts"], i * RING + j - 3)
                for k in range(4):
                    w = bank[5 + j % 2][:, 0:96] if k == 0 else bank[5 + j % 2][:, 96:192]
                    last = nc.scalar.activation(scaled[:, j % 4, k, :], w, ACT.Copy,
                                                scale=shc[:, 4 * j + k:4 * j + k + 1])
                last.then_inc(e_ws, 1)

            def sums_e(i):
                for q in range(2):
                    for jj in range(HALF):
                        j = HALF * q + jj
                        scale_weights(*two_on(i, j))
                        if jj == 0:
                            scalars_out(*next_half(i, q))
                        if jj == 1:
                            silu(*next_half(i, q))
                        sums_out(stage_e, i, j, DM, settled1)

            scalars_out(0, 0)
            silu(0, 0)
            scale_weights(0, 0)
            scale_weights(0, 1)
            looped(act, STEPS, sums_e)

            def transposed_f(n, h, s):
                act.wait_ge(f_T, n + 1)
                wait(act, f_mm, n - 1)
                for b in range(2):
                    last = copy(sumT[:, 2 * s + b, :], bank[2 * s + b][:, 0:3 * NP])
                last.then_inc(f_Ts, 1)

            def finish(n, h, s, following):
                following()
                act.wait_ge(f_var, 2 * n + 2)
                nc.scalar.activation(sd[:, :], mv[:, :, 1], ACT.Sqrt, bias=eps[0:NP, 0:1]).then_inc(f_sd, 1)
                act.wait_ge(f_out, n + 1)
                act.dma_start(pair_rows(out, n), nout[:, s, 0:2 * D]).then_inc(f_st[s], 16)
                if not (isinstance(h, int) and h == NU // 2 - 1):
                    load_pair(act, basetab, n + 2, s, f_base[s])

            for s in range(2):
                load_pair(act, basetab, s, s, f_base[s])
            pipelined(act, NU, transposed_f, finish)


_NAMES = ["x", "src", "dst", "edge_attr_16", "edge_attr_4", "node_vec1", "L0_gnn_wm000", "L0_gnn_wm011",
          "L0_gnn_wm101", "L0_gnn_wm110", "L0_gnn_lm0", "L0_gnn_lm1", "L0_gnn_wu000", "L0_gnn_wu011", "L0_gnn_wu101",
          "L0_gnn_wu110", "L0_gnn_lu0", "L0_gnn_lu1", "L1_gnn_Wfc1", "L1_gnn_Wfc2", "L1_gnn_Wsc0", "L1_gnn_Wsc1",
          "L1_gnn_Wl1_0", "L1_gnn_Wl1_1", "L1_gnn_Wl2_s", "L1_gnn_Wl2_v", "L1_gnn_Wa"]


def kernel(**inputs):
    import numpy as _np
    import concourse.bacc as _bacc
    from concourse import mybir as _mybir
    from concourse.bass_utils import run_bass_kernel_spmd as _run

    nc = _bacc.Bacc("TRN2", target_bir_lowering=False, num_devices=1)
    arrays, args = {}, []
    for name in _NAMES:
        a = _np.ascontiguousarray(inputs[name])
        arrays[f"in_{name}_dram"] = a
        args.append(nc.dram_tensor(f"in_{name}_dram", a.shape, _mybir.dt.from_np(a.dtype), kind="ExternalInput").ap())
    out = nc.dram_tensor("out_dram", (N, D), _mybir.dt.from_np(_np.dtype("float32")), kind="ExternalOutput").ap()
    program(nc, *args, out)
    r = _run(nc, [arrays], core_ids=[0])
    return r.results[0]["out_dram"]
```
